# Optimizing a Trainium2 kernel written in Bass

```python
import numpy as np
import jax
import jax.numpy as jnp

def _softmax(x, axis=-1):
    return jax.nn.softmax(x, axis=axis)

def _gelu(x):
    return jax.nn.gelu(x, approximate=True)

def _silu(x):
    return jax.nn.silu(x)

def _sigmoid(x):
    return jax.nn.sigmoid(x)

def _layernorm(x, axis=-1, eps=1e-05):
    m = jnp.mean(x, axis=axis, keepdims=True)
    v = jnp.var(x, axis=axis, keepdims=True)
    return (x - m) / jnp.sqrt(v + eps)

def _scatter_add(tgt, idx, src, axis=0):
    return tgt.at[idx].add(src)

def _segment_sum(src, seg, n):
    return jax.ops.segment_sum(src, seg, n)
kernel_name = 'mk_adaln_d1_jaxref_r4_73e487'

def setup_inputs(seed: int=0):
    np.random.seed(seed)
    _w = jnp.asarray

    def _L0_attn_setup():
        import jax, jax.numpy as jnp
        import numpy as np
        N_HEAD = 16
        N_KV = 4
        N_EMBD = 512
        HEAD_DIM = N_EMBD // N_HEAD
        GROUP = N_HEAD // N_KV
        key = jax.random.key(seed)
        ks = jax.random.split(key, 5)
        B, S = (2, 512)
        scale = 0.02
        return {'x': jax.random.normal(ks[0], (B, S, N_EMBD), dtype=jnp.float32), 'Wq': jax.random.normal(ks[1], (N_EMBD, N_EMBD), dtype=jnp.float32) * scale, 'Wk': jax.random.normal(ks[2], (N_EMBD, N_EMBD // GROUP), dtype=jnp.float32) * scale, 'Wv': jax.random.normal(ks[3], (N_EMBD, N_EMBD // GROUP), dtype=jnp.float32) * scale, 'Wo': jax.random.normal(ks[4], (N_EMBD, N_EMBD), dtype=jnp.float32) * scale}
    _L0_attn_in = _L0_attn_setup()

    def _L0_ffn_setup():
        import jax, jax.numpy as jnp
        import numpy as np
        E = 8
        TOP_K = 2
        H = 512
        I = 352
        SI = 1408
        key = jax.random.key(seed)
        ks = jax.random.split(key, 9)
        s = lambda fan_in: 1.0 / np.sqrt(fan_in)
        return {'hidden_states': jax.random.normal(ks[0], (4, 512, H), dtype=jnp.float32), 'router_w': jax.random.normal(ks[1], (E, H), dtype=jnp.float32) * s(H), 'w_gate': jax.random.normal(ks[2], (E, H, I), dtype=jnp.float32) * s(H), 'w_up': jax.random.normal(ks[3], (E, H, I), dtype=jnp.float32) * s(H), 'w_down': jax.random.normal(ks[4], (E, I, H), dtype=jnp.float32) * s(I), 'sw_gate': jax.random.normal(ks[5], (H, SI), dtype=jnp.float32) * s(H), 'sw_up': jax.random.normal(ks[6], (H, SI), dtype=jnp.float32) * s(H), 'sw_down': jax.random.normal(ks[7], (SI, H), dtype=jnp.float32) * s(SI), 'shared_gate_w': jax.random.normal(ks[8], (H,), dtype=jnp.float32) * s(H)}
    _L0_ffn_in = _L0_ffn_setup()
    _L0_c = _w((lambda *s: np.random.randn(*s).astype(np.float32) * 0.05)(4, 512))
    _L0_wmod = _w((lambda *s: np.random.randn(*s).astype(np.float32) * 0.05)(512, 6 * 512) * 512 ** (-0.5))
    _d = {'L0_attn_x': _L0_attn_in['x'], 'L0_attn_Wq': _L0_attn_in['Wq'], 'L0_attn_Wk': _L0_attn_in['Wk'], 'L0_attn_Wv': _L0_attn_in['Wv'], 'L0_attn_Wo': _L0_attn_in['Wo'], 'L0_ffn_router_w': _L0_ffn_in['router_w'], 'L0_ffn_w_gate': _L0_ffn_in['w_gate'], 'L0_ffn_w_up': _L0_ffn_in['w_up'], 'L0_ffn_w_down': _L0_ffn_in['w_down'], 'L0_ffn_sw_gate': _L0_ffn_in['sw_gate'], 'L0_ffn_sw_up': _L0_ffn_in['sw_up'], 'L0_ffn_sw_down': _L0_ffn_in['sw_down'], 'L0_ffn_shared_gate_w': _L0_ffn_in['shared_gate_w'], 'L0_c': _L0_c, 'L0_wmod': _L0_wmod}
    _x0 = _d['L0_attn_x']
    _d['L0_attn_x'] = jax.random.normal(jax.random.fold_in(jax.random.key(seed), 1), (4, 1024, 512), dtype=_x0.dtype)
    del _x0
    return _d

def reference(L0_attn_x, L0_attn_Wq, L0_attn_Wk, L0_attn_Wv, L0_attn_Wo, L0_ffn_router_w, L0_ffn_w_gate, L0_ffn_w_up, L0_ffn_w_down, L0_ffn_sw_gate, L0_ffn_sw_up, L0_ffn_sw_down, L0_ffn_shared_gate_w, L0_c, L0_wmod):

    def _L0_attn_ref(x, Wq, Wk, Wv, Wo):
        import jax, jax.numpy as jnp
        import numpy as np
        N_HEAD = 16
        N_KV = 4
        N_EMBD = 512
        HEAD_DIM = N_EMBD // N_HEAD
        GROUP = N_HEAD // N_KV
        B, S, _ = x.shape
        scale = HEAD_DIM ** (-0.5)
        q = (x @ Wq).reshape(B, S, N_KV, GROUP, HEAD_DIM)
        k = (x @ Wk).reshape(B, S, N_KV, HEAD_DIM)
        v = (x @ Wv).reshape(B, S, N_KV, HEAD_DIM)
        scores = jnp.einsum('bqkgd,bskd->bkgqs', q, k) * scale
        causal = jnp.triu(jnp.ones((S, S), dtype=bool), k=1)
        scores = jnp.where(causal, jnp.finfo(scores.dtype).min, scores)
        attn = jax.nn.softmax(scores, axis=-1)
        out = jnp.einsum('bkgqs,bskd->bqkgd', attn, v)
        out = out.reshape(B, S, N_EMBD)
        return out @ Wo

    def _L0_ffn_ref(hidden_states, router_w, w_gate, w_up, w_down, sw_gate, sw_up, sw_down, shared_gate_w):
        import jax, jax.numpy as jnp
        import numpy as np
        E = 8
        TOP_K = 2
        H = 512
        I = 352
        SI = 1408
        B, S, Hd = hidden_states.shape
        x = hidden_states.reshape(-1, Hd)
        shared = jnp.einsum('ts,sh->th', jax.nn.silu(x @ sw_gate) * (x @ sw_up), sw_down)
        logits = x @ router_w.T
        probs = jax.nn.softmax(logits.astype(jnp.float32), axis=-1)
        top_w, top_i = jax.lax.top_k(probs, TOP_K)
        top_w = top_w / jnp.sum(top_w, axis=-1, keepdims=True)
        combine = jnp.sum(jax.nn.one_hot(top_i, E, dtype=x.dtype) * top_w[..., None].astype(x.dtype), axis=1)
        h = jax.nn.silu(jnp.einsum('th,ehi->eti', x, w_gate)) * jnp.einsum('th,ehi->eti', x, w_up)
        expert_out = jnp.einsum('eti,eih->eth', h, w_down)
        routed = jnp.einsum('eth,te->th', expert_out, combine)
        shared_out = jax.nn.sigmoid(x @ shared_gate_w)[:, None] * shared
        return (routed + shared_out).reshape(B, S, Hd)
    x = L0_attn_x
    mod = (_silu(L0_c) @ L0_wmod).reshape(L0_c.shape[0], 6, 1, -1)
    sa, ca, ga, sb, cb, gb = (mod[:, 0], mod[:, 1], mod[:, 2], mod[:, 3], mod[:, 4], mod[:, 5])
    ga = (2 * (ga >= 0) - 1) * jnp.maximum(jnp.abs(ga), 0.25)
    gb = (2 * (gb >= 0) - 1) * jnp.maximum(jnp.abs(gb), 0.25)
    h = _layernorm(x, axis=-1) * (1 + ca) + sa
    x = x + ga * _L0_attn_ref(h, L0_attn_Wq, L0_attn_Wk, L0_attn_Wv, L0_attn_Wo)
    h = _layernorm(x, axis=-1) * (1 + cb) + sb
    x = x + gb * _L0_ffn_ref(h, L0_ffn_router_w, L0_ffn_w_gate, L0_ffn_w_up, L0_ffn_w_down, L0_ffn_sw_gate, L0_ffn_sw_up, L0_ffn_sw_down, L0_ffn_shared_gate_w)
    return x

_drawn_inputs = setup_inputs


def setup_inputs(seed=0):
    import zlib

    import numpy as np

    out = dict(_drawn_inputs(seed))
    spreads = {}
    factors = {'L0_attn_Wq': 8.0,
     'L0_attn_Wk': 8.0,
     'L0_attn_Wv': 8.0,
     'L0_attn_Wo': 8.0,
     'L0_ffn_shared_gate_w': 15.781}
    for name, (base, spread) in spreads.items():
        noise = np.random.default_rng([zlib.crc32(name.encode()), seed]).standard_normal(out[name].shape)
        drawn = base * np.exp(spread * noise) if base else spread * noise
        out[name] = jnp.asarray(drawn.astype(out[name].dtype))
    for name, factor in factors.items():
        out[name] = (out[name] * factor).astype(out[name].dtype)
    return out
```

```python
import concourse.bass as bass
from concourse import mybir
from contextlib import ExitStack

fp32 = mybir.dt.float32
fp16 = mybir.dt.float16
bf16 = mybir.dt.bfloat16
i32 = mybir.dt.int32
u32 = mybir.dt.uint32
ALU = mybir.AluOpType
ACT = mybir.ActivationFunctionType
AX = mybir.AxisListType

B, S, D = 4, 1024, 512
T = B * S
P = 128
KT = D // P
NH, NKV, HD = 16, 4, 32
GH = NH // NKV
E, TOPK, I, SI = 8, 2, 352, 1408
TB = 512
NTB = T // TB
NT = T // P
SUB = TB // P
EPS = 1e-5
WS = 32.0
QKVN = D + 2 * NKV * HD


IT = (I + P - 1) // P
IR = I - (IT - 1) * P
ST = SI // P
RWC = KT * 2 * 2 * I + IT * 2 * D
NX = TOPK * T // P + E - 1
NR = E + 1
N_ATT = B * NKV
XS_EACH = -(-NX // N_ATT)


class Scratch:

    def __init__(self, nc):
        def dram(name, shape, dt):
            return nc.dram_tensor(name, shape, dt, kind="Internal").ap()

        self.mod = dram("mod_s", [B, 6, D], fp32)
        self.q = dram("q_s", [B, NKV, 2, P, S], fp16)
        self.k = dram("k_s", [2, B, P, S], fp16)
        self.v = dram("v_s", [B, NKV, S, HD], fp32)
        self.maxima = dram("max_s", [S // TB, 2, GH * SUB, P], fp16)
        self.xs = dram("xs_s", [N_ATT * XS_EACH, P, D], fp32)
        self.ys = dram("ys_s", [NX * P, D], fp32)
        self.x1 = dram("x1_s", [T // P, P, D], fp32)
        self.h2 = dram("h2_s", [T // P, P, D], fp32)
        self.h2T = dram("h2T_s", [T // P, P, KT, 2, P], fp16)
        self.att = dram("att_s", [B, NKV, 2, P, S], fp16)
        self.sgu = dram("sgu_s", [P, KT, 2, 2, SI], fp16)
        self.sdn = dram("sdn_s", [P, SI // P, 2, D], fp16)


def modulation_and_qkv(nc, a, s):
    NO = 6
    STORES = 5 + NKV
    EXTRA = ST - NTB
    BANKS = 4
    with ExitStack() as ctx:
        def sb(name, shape, dt):
            return ctx.enter_context(nc.sbuf_tensor(name, shape, dt))

        def sem(name):
            return ctx.enter_context(nc.semaphore(name))

        ident = sb("ident1", [P, P], fp32)
        zero = sb("zero1", [P, P], fp32)
        eps = sb("eps1", [P, 1], fp32)
        credit = sb("credit1", [1, 1], fp32)
        cT = sb("cT", [P, KT, B], fp32)
        cth = sb("cth", [P, KT, B], fp32)
        csil = sb("csil", [P, KT, B], fp32)
        wm = sb("wm", [P, KT, 6, D], fp32)
        mod = sb("mod", [B, 6, D], fp32)
        gate = sb("gate", [B, D], fp32)
        gabs = sb("gabs", [B, D], fp32)
        gsgn = sb("gsgn", [B, D], fp32)
        caT = sb("caT", [P, KT, B], fp32)
        saT = sb("saT", [P, KT, B], fp32)
        wst = sb("wst", [P, KT, QKVN], fp32)
        wsp = sb("wsp", [P, KT, 2, QKVN], fp16)
        xt = [sb(f"xt{u}", [P, SUB, D], fp32) for u in range(2)]
        st = sb("st", [P, SUB, 6], fp32)
        mv = sb("mv", [P, SUB, 2], fp32)
        sd = sb("sd", [P, SUB, 1], fp32)
        rs = sb("rs", [P, SUB, 1], fp32)
        zt = sb("zt", [P, SUB, D], fp32)
        h32 = sb("h32", [P, KT, TB], fp32)
        hT = [sb(f"hT{u}", [P, KT, 2, TB], fp16) for u in range(2)]
        qs = [sb(f"qs{u}", [P, 5, 2, TB], fp16) for u in range(2)]
        vs = [sb(f"vs{u}", [P, SUB, P], fp32) for u in range(2)]
        scale = sb("scale1", [P, 1], fp32)
        sws = sb("sws", [P, SI + D], fp32)
        swp = sb("swp", [P, 2, SI + D], fp16)
        pT = [ctx.enter_context(nc.psum_tensor(f"pT{k}", [P, TB], fp32)) for k in range(KT)]
        pO = [ctx.enter_context(nc.psum_tensor(f"pO{k}", [P, TB], fp32)) for k in range(BANKS)]

        c_in, wm_in, wq_in = sem("c_in"), [sem(f"wm_in{j}") for j in range(6)], sem("wq_in")
        ident_set, eps_set = sem("ident_set"), sem("eps_set")
        c_tanh, c_silu, gate_step = sem("c_tanh"), sem("c_silu"), sem("gate_step")
        mod_ps, mod_sb, mod_out, modT_in = sem("mod_ps"), sem("mod_sb"), sem("mod_out"), sem("modT_in")
        w_high, w_low = sem("w_high"), sem("w_low")
        x_in = [sem("x_in0"), sem("x_in1")]
        stats, aggr, sd_ready, rs_ready = sem("stats"), sem("aggr"), sem("sd_ready"), sem("rs_ready")
        z_ready, z_turned, h_ready = sem("z_ready"), sem("z_turned"), sem("h_ready")
        h_high, h_low = sem("h_high"), sem("h_low")
        o_ps, o_high, o_read = sem("o_ps"), sem("o_high"), sem("o_read")
        q_stored = [sem("q_stored0"), sem("q_stored1")]
        sw_in, sw_step, sw_stored, scale_set = sem("sw_in"), sem("sw_step"), sem("sw_stored"), sem("scale_set")

        x_v = a["L0_attn_x"].rearrange("b (n s p) d -> (b n) p s d", s=SUB, p=P)
        with nc.Block() as block:
            @block.sync
            def _(sp):
                for k in range(KT):
                    sp.dma_start(cT[:, k, :], a["L0_c"][:, k * P:(k + 1) * P].rearrange("b p -> p b"),
                                 allow_slow_non_contiguous=True).then_inc(c_in, 16)
                wm_v = a["L0_wmod"].rearrange("(k p) (j d) -> p k j d", p=P, j=6)
                for j in range(2):
                    sp.dma_start(wm[:, :, j, :], wm_v[:, :, j, :]).then_inc(wm_in[j], 16)
                for u in range(2):
                    sp.dma_start(xt[u][:, :, :], x_v[u, :, :, :]).then_inc(x_in[u], 16)
                for w, at, n in (("Wq", 0, D), ("Wk", D, P), ("Wv", D + P, P)):
                    sp.dma_start(wst[:, :, at:at + n],
                                 a["L0_attn_" + w].rearrange("(k p) n -> p k n", p=P)).then_inc(wq_in, 16)
                for j in range(2, 6):
                    sp.dma_start(wm[:, :, j, :], wm_v[:, :, j, :]).then_inc(wm_in[j], 16)

                def load_shared(n, k, w):
                    sp.dma_start(sws[:, 0:SI], a["L0_ffn_sw_" + ("gate", "up")[w]].rearrange("(k p) c -> p k c", p=P)
                                 [:, bass.ds(k, 1), :].rearrange("p k c -> p (k c)")).then_inc(sw_in, 16)
                    sp.dma_start(sws[:, SI:], sdn_v[:, bass.ds(n, 1), :].rearrange("p k c -> p (k c)")).then_inc(sw_in, 16)

                sdn_v = a["L0_ffn_sw_down"].rearrange("(k p) c -> p k c", p=P)
                sp.dma_start(sws[:, 0:EXTRA * D].rearrange("p (k c) -> p k c", k=EXTRA), sdn_v[:, NTB:, :]).then_inc(sw_in, 16)
                sp.wait_ge(mod_sb, 2)
                sp.dma_start(s.mod[:, 0:2, :], mod[:, 0:2, :]).then_inc(mod_out, 16)
                sp.wait_ge(mod_out, 16)
                for k in range(KT):
                    for j, to in ((0, saT), (1, caT)):
                        sp.dma_start(to[:, k, :], s.mod[:, j, k * P:(k + 1) * P].rearrange("b p -> p b"),
                                     allow_slow_non_contiguous=True)\
                          .then_inc(modT_in, 16)

                sp.wait_ge(sw_step, 3)
                for hl in range(2):
                    sp.dma_start(s.sdn[:, NTB:, hl, :], swp[:, hl, 0:EXTRA * D].rearrange("p (k c) -> p k c", k=EXTRA))\
                      .then_inc(sw_stored, 16)
                load_shared(0, 0, 0)

                def tiles(b, last):
                    for u in range(2):
                        n = b * 2 + u if last else sp.snap(b * 2 + u)
                        for r in range(NO):
                            if r == 3:
                                sp.wait_ge(sw_step, (n + 2) * 3)
                                sp.dma_start(s.sgu[:, bass.ds(b, 1), u, :, :].rearrange("p o h c -> p (o h) c"),
                                             swp[:, :, 0:SI]).then_inc(sw_stored, 16)
                                sp.dma_start(s.sdn[:, bass.ds(n, 1), :, :].rearrange("p o h c -> p (o h) c"),
                                             swp[:, :, SI:]).then_inc(sw_stored, 16)
                                if not (last and u == 1):
                                    load_shared(n + 1, b + u, 1 - u)
                            if r == NKV:
                                continue
                            sp.wait_ge(o_read, n * NO + (r + 1 + BANKS))
                            tok = slice(u * TB, (u + 1) * TB)
                            if r < NKV:
                                sp.dma_start(s.q[bass.ds(b, 1), r, :, :, tok].rearrange("o h p t -> p (o h) t"),
                                             qs[u][:, r, :, :]).then_inc(q_stored[u], 16)
                            else:
                                sp.dma_start(s.k[:, bass.ds(b, 1), :, tok].rearrange("h o p t -> p (o h) t"),
                                             qs[u][:, NKV, :, :]).then_inc(q_stored[u], 16)
                                for g in range(NKV):
                                    sp.dma_start(s.v[bass.ds(b, 1), g, tok, :].rearrange("o (s p) c -> p (o s) c", p=P),
                                                 vs[u][:, :, g * HD:(g + 1) * HD]).then_inc(q_stored[u], 16)

                with sp.Fori(0, B - 1) as b:
                    tiles(b, False)
                tiles(B - 1, True)
                sp.wait_ge(mod_sb, 6)
                sp.dma_start(s.mod[:, 2:6, :], mod[:, 2:6, :]).then_inc(mod_out, 16)
                sp.wait_ge(mod_out, 32)
                sp.wait_ge(sw_stored, (NTB + 1) * 32)
                for u in range(2):
                    sp.wait_ge(q_stored[u], B * STORES * 16)

            @block.gpsimd
            def _(pool):
                pool.memset(eps[:, :], EPS).then_inc(eps_set, 1)
                pool.memset(zero[:, :], 0.0).then_inc(ident_set, 1)
                pool.wait_ge(ident_set, 1)
                pool.affine_select(out=ident[:, :], in_=zero[:, :], compare_op=ALU.not_equal, fill=1.0,
                                   base=0, pattern=[[-1, P]], channel_multiplier=1).then_inc(ident_set, 1)
                pool.memset(scale[:, :], WS).then_inc(scale_set, 1)
                pool.wait_ge(scale_set, 1)

                def split_shared(j, width):
                    by = scale[:, :].to_broadcast([P, width])
                    pool.tensor_tensor(swp[:, 0, 0:width], sws[:, 0:width], by, ALU.mult).then_inc(sw_step, 1)
                    pool.wait_ge(sw_step, j * 3 + 1)
                    pool.tensor_tensor(sws[:, 0:width], sws[:, 0:width], by, ALU.mult).then_inc(sw_step, 1)
                    pool.wait_ge(sw_step, j * 3 + 2)
                    pool.tensor_tensor(swp[:, 1, 0:width], sws[:, 0:width], swp[:, 0, 0:width], ALU.subtract)\
                        .then_inc(sw_step, 1)

                pool.wait_ge(sw_in, 16)
                split_shared(0, EXTRA * D)

                with pool.Fori(0, B) as b:
                    for u in range(2):
                        for k in range(KT):
                            pool.wait_ge(h_high, (b * 2 + u) * KT + (k + 1))
                            pool.tensor_tensor(hT[u][:, k, 1, :], h32[:, k, :], hT[u][:, k, 0, :],
                                               ALU.subtract).then_inc(h_low, 1)
                        pool.wait_ge(sw_stored, (b * 2 + (u + 1)) * 32)
                        pool.wait_ge(sw_in, (b * 2 + (u + 1)) * 32 + 16)
                        split_shared(b * 2 + (u + 1), SI + D)

            @block.tensor
            def _(pe):
                def modulation(jj):
                    for j in jj:
                        pe.wait_ge(wm_in[j], 16)
                        for k in range(KT):
                            mm = pe.matmul(pT[j % KT][0:B, :], csil[:, k, :], wm[:, k, j, :],
                                           start=k == 0, stop=k == KT - 1)
                        mm.then_inc(mod_ps, 1)

                def turn(n):
                    for i in range(SUB):
                        pe.wait_ge(z_ready, n * SUB + (i + 1))
                        for k in range(KT):
                            mm = pe.transpose(pT[k][:, i * P:(i + 1) * P], zt[:, i, k * P:(k + 1) * P],
                                              ident[:, :])
                        mm.then_inc(z_turned, 1)

                def result(n, u, r):
                    if r == 0:
                        pe.wait_ge(h_low, (n + 1) * KT)
                    pe.wait_ge(o_read, n * NO + (r + 1))
                    out = pO[(NO * u + r) % BANKS]
                    if r < 5:
                        for k in range(KT):
                            for wl, hl in ((0, 0), (0, 1), (1, 0)):
                                mm = pe.matmul(out[:, :], wsp[:, k, wl, r * P:(r + 1) * P], hT[u][:, k, hl, :],
                                               start=k == 0 and (wl, hl) == (0, 0),
                                               stop=k == KT - 1 and wl == 1)
                    else:
                        for i in range(SUB):
                            for k in range(KT):
                                for hl, wl in ((0, 0), (0, 1), (1, 0)):
                                    mm = pe.matmul(out[:, i * P:(i + 1) * P], hT[u][:, k, hl, i * P:(i + 1) * P],
                                                   wsp[:, k, wl, 5 * P:6 * P],
                                                   start=k == 0 and (hl, wl) == (0, 0),
                                                   stop=k == KT - 1 and hl == 1)
                    mm.then_inc(o_ps, 1)

                def tile(n, u, last):
                    for r in range(3):
                        result(n, u, r)
                    if not last:
                        turn(n + 1)
                    for r in range(3, NO):
                        result(n, u, r)

                pe.wait_ge(c_silu, 2)
                modulation((0, 1))
                pe.wait_ge(ident_set, 2)
                pe.wait_ge(mod_sb, 2)
                turn(0)
                pe.wait_ge(w_low, 1)
                with pe.Fori(0, B - 1) as b:
                    tile(b * 2, 0, False)
                    tile(b * 2 + 1, 1, False)
                tile(2 * B - 2, 0, False)
                tile(2 * B - 1, 1, True)
                modulation((2, 3, 4, 5))

            @block.scalar
            def _(act):
                act.wait_ge(c_in, KT * 16)
                act.activation(cth[:, :, :], cT[:, :, :], ACT.Tanh, scale=0.5).then_inc(c_tanh, 1)
                act.wait_ge(wq_in, 48)
                act.activation(wsp[:, :, 0, :], wst[:, :, :], ACT.Copy, scale=WS).then_inc(w_high, 1)
                act.wait_ge(eps_set, 1)

                def deviation(n):
                    act.wait_ge(aggr, n + 1)
                    act.activation(sd[:, :, 0], mv[:, :, 1], ACT.Sqrt, bias=eps[:, :]).then_inc(sd_ready, 1)

                def high_parts(n, u):
                    for k in range(KT):
                        act.wait_ge(h_ready, n * KT + (k + 1))
                        act.activation(hT[u][:, k, 0, :], h32[:, k, :], ACT.Copy).then_inc(h_high, 1)

                def results(n, b, u, rr):
                    for r in rr:
                        act.wait_ge(o_ps, n * NO + (r + 1))
                        if r == 0:
                            act.wait_ge(q_stored[u], b * (STORES * 16))
                        act.activation(qs[u][:, r, 0, :], pO[(NO * u + r) % BANKS][:, :], ACT.Copy,
                                       scale=1 / WS).then_inc(o_high, 1)

                def tile(n, b, u, last, more=True):
                    if more:
                        act.wait_ge(z_ready, (n + 1) * SUB)
                        act.dma_start(xt[u][:, :, :], x_v[bass.ds(n + 2, 1), :, :, :]
                                      .rearrange("o p s d -> p (o s) d")).then_inc(x_in[u], 16)
                    if not last:
                        deviation(n + 1)
                    results(n, b, u, range(3))
                    if not last:
                        high_parts(n + 1, 1 - u)
                    results(n, b, u, range(3, 5))

                deviation(0)
                high_parts(0, 0)
                with act.Fori(0, B - 1) as b:
                    tile(b * 2, b, 0, False)
                    tile(b * 2 + 1, b, 1, False)
                tile(2 * B - 2, B - 1, 0, False, False)
                tile(2 * B - 1, B - 1, 1, True, False)

            @block.vector
            def _(dve):
                dve.memset(credit[:, :], 0.0).then_inc(o_read, BANKS)
                dve.wait_ge(c_tanh, 1)
                dve.scalar_tensor_tensor(cth[:, :, :], cth[:, :, :], 1.0, cT[:, :, :], ALU.add, ALU.mult)\
                   .then_inc(c_silu, 1)
                dve.wait_ge(c_silu, 1)
                dve.tensor_scalar(csil[:, :, :], cth[:, :, :], 0.5, None, ALU.mult).then_inc(c_silu, 1)

                def normalise(n, b, u):
                    dve.wait_ge(x_in[u], (b + 1) * 16)
                    for i in range(SUB):
                        op = dve.bn_stats(st[:, i, :], xt[u][:, i, :])
                    op.then_inc(stats, 1)
                    dve.wait_ge(sd_ready, n)
                    dve.wait_ge(stats, n + 1)
                    for i in range(SUB):
                        if i == 0:
                            dve.tensor_copy(credit[:, :], credit[:, :])
                        op = dve.bn_aggr(mv[:, i, :], st[:, i, :])
                    op.then_inc(aggr, 1)
                    dve.wait_ge(sd_ready, n + 1)
                    dve.reciprocal(rs[:, :, :], sd[:, :, :]).then_inc(rs_ready, 1)
                    dve.wait_ge(rs_ready, n + 1)
                    for i in range(SUB):
                        dve.tensor_scalar(zt[:, i, :], xt[u][:, i, :], mv[:, i, 0:1], rs[:, i, 0:1],
                                          ALU.subtract, ALU.mult).then_inc(z_ready, 1)

                def modulate(n, b):
                    dve.wait_ge(z_turned, (n + 1) * SUB)
                    for k in range(KT):
                        dve.tensor_scalar(h32[:, k, :], pT[k][:, :], caT[:, k, bass.ds(b, 1)], saT[:, k, bass.ds(b, 1)],
                                          ALU.mult, ALU.add).then_inc(h_ready, 1)

                def results(n, u, rr):
                    for r in rr:
                        out = pO[(NO * u + r) % BANKS]
                        if r < 5:
                            dve.wait_ge(o_high, n * 5 + (r + 1))
                            dve.scalar_tensor_tensor(qs[u][:, r, 1, :], out[:, :], 1 / WS, qs[u][:, r, 0, :],
                                                     ALU.mult, ALU.subtract).then_inc(o_read, 1)
                        else:
                            dve.wait_ge(o_ps, n * NO + (r + 1))
                            dve.tensor_scalar(vs[u][:, :, :], out[:, :].rearrange("p (s c) -> p s c", s=SUB),
                                              1 / WS, None, ALU.mult).then_inc(o_read, 1)

                def tile(n, b, u, last):
                    if not last:
                        normalise(n + 1, b + u, 1 - u)
                    results(n, u, range(3))
                    if not last:
                        modulate(n + 1, b + u)
                    results(n, u, range(3, NO))

                normalise(0, 0, 0)
                for j in range(2):
                    dve.wait_ge(mod_ps, j + 1)
                    dve.tensor_scalar(mod[:, j, :], pT[j][0:B, :], float(j), None, ALU.add).then_inc(mod_sb, 1)
                dve.wait_ge(w_high, 1)
                dve.scalar_tensor_tensor(wsp[:, :, 1, :], wst[:, :, :], WS, wsp[:, :, 0, :],
                                         ALU.mult, ALU.subtract).then_inc(w_low, 1)
                dve.wait_ge(modT_in, 2 * KT * 16)
                modulate(0, 0)
                with dve.Fori(0, B - 1) as b:
                    tile(b * 2, b, 0, False)
                    tile(b * 2 + 1, b, 1, False)
                tile(2 * B - 2, B - 1, 0, False)
                tile(2 * B - 1, B - 1, 1, True)
                for step, j in enumerate((2, 5)):
                    dve.wait_ge(mod_ps, j + 1)
                    dve.tensor_copy(gate[:, :], pT[j % KT][0:B, :]).then_inc(gate_step, 1)
                    dve.wait_ge(gate_step, 4 * step + 1)
                    dve.scalar_tensor_tensor(gabs[:, :], gate[:, :], -1.0, gate[:, :], ALU.mult, ALU.max)\
                       .then_inc(gate_step, 1)
                    dve.tensor_scalar(gsgn[:, :], gate[:, :], 0.0, 2.0, ALU.is_ge, ALU.mult).then_inc(gate_step, 1)
                    dve.wait_ge(gate_step, 4 * step + 3)
                    dve.tensor_scalar(gabs[:, :], gabs[:, :], 0.25, None, ALU.max).then_inc(gate_step, 1)
                    dve.wait_ge(gate_step, 4 * step + 4)
                    dve.scalar_tensor_tensor(mod[:, j, :], gsgn[:, :], -1.0, gabs[:, :], ALU.add, ALU.mult)\
                       .then_inc(mod_sb, 1)
                for j in (3, 4):
                    dve.tensor_scalar(mod[:, j, :], pT[j % KT][0:B, :], float(j - 3), None, ALU.add).then_inc(mod_sb, 1)


def routed_layout(rw):
    gu = KT * 2 * 2 * I
    return (rw[:, :, 0:gu].rearrange("p e (k h w i) -> p e k h w i", k=KT, h=2, w=2),
            rw[:, :, gu:].rearrange("p e (k h d) -> p e k h d", k=IT, h=2))


def attention(nc, a, s, rw):
    SCALE = HD ** -0.5
    NEG = -1e30
    HALF = S // TB
    KEYS = S // P
    ROWS = 3 * HD
    STEPS = [(c, j) for c in range(HALF) for j in range((c + 1) * SUB)]
    NS = len(STEPS)
    N = B * NKV
    PIECES = 8
    START = 2
    PRE = 2

    def cols(k):
        c, j = STEPS[k]
        off = max(0, j - c * SUB) * P
        return c, j, off, TB - off

    tasks = []
    for c in range(HALF):
        for i in range(c * SUB, (c + 1) * SUB):
            for h in range(GH):
                for k0 in range(0, (i + 1) * P, TB):
                    n = min(TB, (i + 1) * P - k0)
                    tasks.append((c, h, i, k0, n, k0 + n == (i + 1) * P))
        tasks.append((c,))
    NTASK = len(tasks)
    TURN = [t for t, x in enumerate(tasks) if len(x) == 1]
    share, beside, done = [0 if k < START else cols(k)[3] + 200 for k in range(NS)], [], 0
    cost = [x[4] + 130 if len(x) > 1 else 400 for x in tasks]
    for k in range(NS):
        upto = sum(share[:k + 1]) / sum(share) * sum(cost)
        now = []
        while done < NTASK and sum(cost[:done + 1]) <= upto + 1:
            now.append(done)
            done += 1
        beside.append(now)
    assert done == NTASK

    with ExitStack() as ctx:
        def sb(name, shape, dt):
            return ctx.enter_context(nc.sbuf_tensor(name, shape, dt))

        def sem(name):
            return ctx.enter_context(nc.semaphore(name))

        qst = [sb(f"qst{u}", [P, GH, S], fp16) for u in range(2)]
        kst = [sb(f"kst{u}", [P, S], fp16) for u in range(2)]
        vt = [sb(f"vt{u}", [P, KEYS, HD], fp32) for u in range(2)]
        pb = [sb(f"pb{u}", [P, GH, TB], fp32) for u in range(2)]
        rec = sb("rec", [P, TB], fp32)
        o32 = [sb(f"o32{c}", [P, TB], fp32) for c in range(HALF)]
        ohl = [sb(f"ohl{c}", [P, 2, TB], fp16) for c in range(HALF)]
        gust = sb("gust", [P, 2, KT, I], fp32)
        dnst = sb("dnst", [P, IT, D], fp32)
        ident = sb("ident2", [P, P], fp32)
        identb = sb("identb2", [P, P], bf16)
        mask_m = sb("mask_m", [P, P], bf16)
        mask_s = sb("mask_s", [P, P], bf16)
        zero = sb("zero2", [P, P], bf16)
        ones = sb("ones2", [P, HD], fp32)
        scale = sb("scale2", [P, 1], fp32)
        one = sb("one2", [P, 1], fp32)
        gate_op = sb("gate_op", [P, 1], fp32)
        clear = sb("clear", [P, P], fp32)
        mxp = sb("mxp", [P, 2, GH * SUB], fp32)
        mx = [sb(f"mx{c}", [P, GH * SUB], fp32) for c in range(HALF)]
        mrow = [sb(f"mrow{c}", [GH * SUB, 2, P], fp16) for c in range(HALF)]
        pS = [ctx.enter_context(nc.psum_tensor(f"pS{x}", [P, 2, TB], fp32)) for x in range(2)]
        pM = [ctx.enter_context(nc.psum_tensor(f"pM{x}", [P, TB], fp32)) for x in range(PRE)]
        pA = ctx.enter_context(nc.psum_tensor("pA", [P, TB], fp32))
        pD = ctx.enter_context(nc.psum_tensor("pD", [P, TB], fp32))

        consts = sem("consts2")
        qk_in, v_in = [sem("qk_in0"), sem("qk_in1")], [sem("v_in0"), sem("v_in1")]
        m_ps, m_read, m_neg, mx_ready = sem("m_ps"), sem("m_read"), sem("m_neg"), sem("mx_ready")
        max_out = sem("max_out")
        max_in = [sem(f"max_in{c}") for c in range(HALF)]
        s_ps, p_ready, p_free = sem("s_ps"), sem("p_ready"), sem("p_free")
        acc_read, rec_ready, o_ready, o_split = sem("acc_read"), sem("rec_ready"), sem("o_ready"), sem("o_split")
        att_out = [sem(f"att_out{c}") for c in range(HALF)]
        gu_in, dn_in, gu_step, dn_step = sem("gu_in"), sem("dn_in"), sem("gu_step"), sem("dn_step")
        clear_set, xs_clear = sem("clear_set"), sem("xs_clear")
        NCONST = 11
        LOADS = 6

        q_v = s.q.rearrange("b g h p t -> (b g) h p t")
        a_v = s.att.rearrange("b g h p t -> (b g) h p t")
        k_v = s.k.rearrange("h b (g p) t -> h (b g) p t", g=NKV)
        v_v = s.v.rearrange("b g (j p) c -> (b g) p j c", p=P)
        rgu, rdn = routed_layout(rw)

        with nc.Block() as block:
            @block.sync
            def _(sp):
                def load_qk(n, u):
                    for at, hl in ((0, 0), (1, 1), (2, 0)):
                        sp.dma_start(qst[u][at * HD:(at + 1) * HD, :, :],
                                     q_v[bass.ds(n, 1), hl, :, :].rearrange("o (h p) t -> p (o h) t", p=HD))\
                          .then_inc(qk_in[u], 16)
                    for at, hl in ((0, 0), (1, 0), (2, 1)):
                        sp.dma_start(kst[u][at * HD:(at + 1) * HD, :],
                                     k_v[hl, bass.ds(n, 1), :, :].rearrange("o p t -> p (o t)")).then_inc(qk_in[u], 16)

                def load_v(n, u):
                    for j in (KEYS // 2, 0):
                        sp.dma_start(vt[u][:, j:j + KEYS // 2, :], v_v[bass.ds(n, 1), :, j:j + KEYS // 2, :]
                                     .rearrange("o p j c -> p (o j) c")).then_inc(v_in[u], 16)

                def load_gate_up(e):
                    for w, name in enumerate(("w_gate", "w_up")):
                        sp.dma_start(gust[:, w, :, :], a["L0_ffn_" + name][bass.ds(e, 1), :, :]
                                     .rearrange("o (k p) i -> p (o k) i", p=P)).then_inc(gu_in, 16)

                def load_down(e):
                    w = a["L0_ffn_w_down"]
                    sp.dma_start(dnst[:, 0:IT - 1, :], w[bass.ds(e, 1), 0:(IT - 1) * P, :]
                                 .rearrange("o (k p) d -> p (o k) d", p=P)).then_inc(dn_in, 16)
                    sp.dma_start(dnst[0:IR, IT - 1, :], w[bass.ds(e, 1), (IT - 1) * P:, :]
                                 .rearrange("o p d -> p (o d)")).then_inc(dn_in, 16)

                def rows_out(n, c):
                    sp.wait_ge(m_read, n * NTASK + (TURN[c] + 1 + PRE))
                    sp.dma_start(s.maxima[c, :, :, :].rearrange("r q p -> q r p"), mrow[c][:, :, :]).then_inc(max_out, 16)

                def rows_in(n, u, c):
                    sp.wait_ge(max_out, n * 32 + (c + 1) * 16)
                    sp.dma_start(qst[u][ROWS:ROWS + 2, :, c * TB:(c + 1) * TB],
                                 s.maxima[c, :, :, :].rearrange("r (h i) p -> r h (i p)", h=GH)).then_inc(max_in[c], 16)

                def step(n, u, m, left):
                    if left > 0:
                        sp.wait_ge(p_free, n * NS + PRE)
                        load_v(n + 1, 1 - u)
                    if u == 0:
                        sp.wait_ge(dn_step, m * 6)
                        load_down(m)
                    elif left > 0:
                        sp.wait_ge(gu_step, (m + 1) * 6)
                        load_gate_up(m + 1)
                    sp.dma_start(s.xs.rearrange("j p d -> (j p d)")[bass.ds(n * (XS_EACH * P * D), XS_EACH * P * D)]
                                 .rearrange("(p r c) -> p r c", p=P, c=P),
                                 clear[:, :].rearrange("p (o d) -> p o d", o=1).to_broadcast([P, XS_EACH * KT, P]))\
                      .then_inc(xs_clear, 16)
                    if left > 0:
                        rows_out(n + 1, 0)
                        rows_in(n + 1, 1 - u, 0)
                        rows_out(n + 1, 1)
                        if left > 1:
                            sp.wait_ge(s_ps, (n + 1) * (2 * NS))
                            load_qk(n + 2, u)
                        rows_in(n + 1, 1 - u, 1)

                load_qk(0, 0)
                load_v(0, 0)
                load_qk(1, 1)
                load_gate_up(0)
                sp.wait_ge(clear_set, 1)
                for c in range(HALF):
                    rows_out(0, c)
                    rows_in(0, 0, c)
                with sp.Fori(0, N // 2 - 1) as m:
                    step(m * 2, 0, m, 2)
                    step(m * 2 + 1, 1, m, 2)
                step(N - 2, 0, N // 2 - 1, 1)
                step(N - 1, 1, N // 2 - 1, 0)
                sp.wait_ge(xs_clear, N * 16)

            @block.gpsimd
            def _(pool):
                for t, value in ((zero, 0.0), (ones, 1.0), (scale, WS), (one, 1.0), (gate_op, 0.0)):
                    pool.memset(t[:, :], value).then_inc(consts, 1)
                pool.wait_ge(consts, 7)
                for t in (ident, identb):
                    pool.affine_select(out=t[:, :], in_=zero[:, :], compare_op=ALU.not_equal, fill=1.0,
                                       base=0, pattern=[[-1, P]], channel_multiplier=1).then_inc(consts, 1)
                pool.affine_select(out=mask_m[:, :], in_=zero[:, :], compare_op=ALU.is_ge, fill=NEG,
                                   base=0, pattern=[[-1, P]], channel_multiplier=1).then_inc(consts, 1)
                pool.affine_select(out=mask_s[:, :], in_=zero[:, :], compare_op=ALU.is_ge, fill=NEG,
                                   base=0, pattern=[[1, P]], channel_multiplier=-1).then_inc(consts, 1)
                pool.tensor_tensor(gate_op[:, :], one[:, :], one[:, :], ALU.mult).then_inc(o_split, 2 * HALF)

                def split(e, parts, step, base):
                    for x, (src, hi, lo) in enumerate(parts):
                        by = scale[0:src.shape[0], :].to_broadcast(list(src.shape))
                        pool.tensor_tensor(hi, src, by, ALU.mult).then_inc(step, 1)
                    for x, (src, hi, lo) in enumerate(parts):
                        pool.wait_ge(step, base + (x + 1))
                        by = scale[0:src.shape[0], :].to_broadcast(list(src.shape))
                        pool.tensor_tensor(src, src, by, ALU.mult).then_inc(step, 1)
                    for x, (src, hi, lo) in enumerate(parts):
                        pool.wait_ge(step, base + (x + 3))
                        pool.tensor_tensor(lo, src, hi, ALU.subtract).then_inc(step, 1)

                def split_gate_up(e):
                    pool.wait_ge(gu_in, e * 32 + 32)
                    split(e, [(gust[:, w, :, :], rgu[:, bass.ds(e, 1), :, 0, w, :].rearrange("p o k i -> p (o k) i"),
                               rgu[:, bass.ds(e, 1), :, 1, w, :].rearrange("p o k i -> p (o k) i")) for w in range(2)],
                          gu_step, e * 6)

                def split_down(e):
                    pool.wait_ge(dn_in, e * 32 + 32)
                    split(e, [(dnst[:, 0:IT - 1, :], rdn[:, bass.ds(e, 1), 0:IT - 1, 0, :].rearrange("p o k i -> p (o k) i"),
                               rdn[:, bass.ds(e, 1), 0:IT - 1, 1, :].rearrange("p o k i -> p (o k) i")),
                              (dnst[0:IR, IT - 1, :], rdn[0:IR, bass.ds(e, 1), IT - 1, 0, :].rearrange("p o i -> p (o i)"),
                               rdn[0:IR, bass.ds(e, 1), IT - 1, 1, :].rearrange("p o i -> p (o i)"))],
                          dn_step, e * 6)

                def split_output(n, c):
                    base = n * 2 * HALF + (2 * c + 2 * HALF)
                    by = one[:, :].to_broadcast([P, TB])
                    pool.wait_ge(att_out[c], n * 16)
                    pool.wait_ge(o_ready, n * HALF + (c + 1))
                    pool.tensor_tensor(ohl[c][:, 0, :], o32[c][:, :], by, ALU.mult).then_inc(o_split, 1)
                    pool.wait_ge(o_split, base + 1)
                    pool.tensor_tensor(ohl[c][:, 1, :], o32[c][:, :], ohl[c][:, 0, :], ALU.subtract).then_inc(o_split, 1)
                    pool.wait_ge(o_split, base + 2)
                    pool.tensor_tensor(gate_op[:, :], one[:, :], one[:, :], ALU.mult).then_inc(consts, 1)
                    pool.dma_start(a_v[bass.ds(n, 1), :, :, c * TB:(c + 1) * TB].rearrange("o h p t -> p (o h) t"),
                                   ohl[c][:, :, :]).then_inc(att_out[c], 16)

                with pool.Fori(0, N // 2) as m:
                    split_gate_up(m)
                    split_output(m * 2, 0)
                    split_output(m * 2, 1)
                    split_down(m)
                    split_output(m * 2 + 1, 0)
                    split_output(m * 2 + 1, 1)
                for c in range(HALF):
                    pool.wait_ge(att_out[c], N * 16)

            @block.tensor
            def _(pe):
                def maximum(n, u, t):
                    x = tasks[t]
                    out = pM[t % PRE]
                    if len(x) == 1:
                        c = x[0]
                        if c == 0:
                            pe.wait_ge(m_read, n * NTASK + (t + PRE))
                        else:
                            pe.wait_ge(mx_ready, n + 1)
                            pe.wait_ge(m_read, n * NTASK + (t + 1))
                        pe.transpose(out[0:GH * SUB, 0:P], mx[c][:, :], ident[:, :]).then_inc(m_ps, 1)
                        return
                    c, h, i, k0, w, diagonal = x
                    pe.wait_ge(m_read, n * NTASK + (t + 1))
                    mm = pe.matmul(out[:, 0:w], qst[u][0:ROWS, h, i * P:(i + 1) * P], kst[u][0:ROWS, k0:k0 + w],
                                   start=True, stop=not diagonal)
                    if diagonal:
                        mm = pe.matmul(out[:, w - P:w], identb[:, :], mask_m[:, :], start=False, stop=True)
                    mm.then_inc(m_ps, 1)

                def scores(n, u, k, x):
                    c, j, off, w = cols(k)
                    if x == 0 and j == 0:
                        pe.wait_ge(max_in[c], n * 16 + 16)
                    if not (k == 0 and isinstance(n, int) and n == 0):
                        pe.wait_ge(p_ready, n * (2 * NS) + (2 * k - 1 + x))
                    for y in range(2):
                        mm = pe.matmul(pS[x][:, y, 0:w], kst[u][0:ROWS + 2, j * P:(j + 1) * P],
                                       qst[u][0:ROWS + 2, 2 * x + y, c * TB + off:(c + 1) * TB],
                                       start=True, stop=j < c * SUB)
                        if j >= c * SUB:
                            mm = pe.matmul(pS[x][:, y, 0:P], identb[:, :], mask_s[:, :], start=False, stop=True)
                    mm.then_inc(s_ps, 1)

                def values(n, u, k, what):
                    c, j, off, w = cols(k)
                    first, last = j == 0, j == (c + 1) * SUB - 1
                    if what == 0:
                        pe.wait_ge(p_ready, n * (2 * NS) + (2 * k + 2))
                    if k == 0 and what == 0:
                        pe.wait_ge(v_in[u], steps_done * 32)
                    if first:
                        pe.wait_ge(acc_read, n * (2 * HALF) + (2 * c + what))
                    out, lhs = (pA, vt[u][:, j, :]) if what == 0 else (pD, ones[:, :])
                    for h in range(GH):
                        mm = pe.matmul(out[h * HD:(h + 1) * HD, off:TB], lhs, pb[k % 2][:, h, 0:w],
                                       start=first, stop=last)
                    if what == 1:
                        mm.then_inc(p_free, 1)

                def step(n, u, last):
                    for k in range(NS):
                        todo = [] if last else beside[k]
                        if k == START and not last:
                            pe.wait_ge(qk_in[1 - u], (steps_done + u) * (LOADS * 16))
                        for x in range(4):
                            if x < 2 and k + 1 < NS:
                                scores(n, u, k + 1, x)
                            elif x < 2 and not last:
                                scores(n + 1, 1 - u, 0, x)
                            elif x >= 2:
                                values(n, u, k, x - 2)
                            for t in todo[len(todo) * x // 4:len(todo) * (x + 1) // 4]:
                                maximum(n + 1, 1 - u, t)

                pe.wait_ge(consts, NCONST)
                pe.wait_ge(qk_in[0], LOADS * 16)
                for t in range(NTASK):
                    maximum(0, 0, t)
                for x in range(2):
                    scores(0, 0, 0, x)
                with pe.Fori(0, N // 2 - 1) as m:
                    steps_done = m + 1
                    step(m * 2, 0, False)
                    step(m * 2 + 1, 1, False)
                steps_done = N // 2
                step(N - 2, 0, False)
                step(N - 1, 1, True)

            @block.scalar
            def _(act):
                def step(n, first=False):
                    for k in range(NS):
                        c, j, off, w = cols(k)
                        act.wait_ge(p_free, n * NS + (k + 1))
                        for x in range(2):
                            act.wait_ge(s_ps, n * (2 * NS) + (2 * k + x + 1))
                            act.activation(pb[k % 2][:, 2 * x:2 * x + 2, 0:w], pS[x][:, :, 0:w], ACT.Exp,
                                           scale=SCALE).then_inc(p_ready, 1)
                        if k == 0 and not first:
                            leave_psum(n - 1, 1)
                        if k == SUB:
                            leave_psum(n, 0)

                def leave_psum(n, c):
                    k = NS if c == HALF - 1 else SUB
                    act.wait_ge(p_free, n * NS + (k + PRE))
                    act.wait_ge(o_split, n * (2 * HALF) + (2 * c + 2))
                    act.activation(o32[c][:, :], pA[:, :], ACT.Copy).then_inc(acc_read, 1)
                    act.wait_ge(o_ready, n * HALF + c)
                    act.activation(rec[:, :], pD[:, :], ACT.Copy).then_inc(acc_read, 1)

                step(0, True)
                with act.Fori(1, N) as n:
                    step(n)
                leave_psum(N - 1, 1)

            @block.vector
            def _(dve):
                dve.memset(clear[:, :], 0.0).then_inc(clear_set, 1)
                for u in range(2):
                    dve.memset(kst[u][ROWS:ROWS + 2, :], 1.0).then_inc(consts, 1)
                dve.memset(rec[:, 0:1], 0.0).then_inc(m_read, PRE)
                dve.memset(rec[:, 1:2], 0.0).then_inc(p_free, PRE)
                dve.memset(rec[:, 2:3], 0.0).then_inc(acc_read, 1)

                def maximum(n, t):
                    x = tasks[t]
                    src = pM[t % PRE]
                    if len(x) == 1:
                        c = x[0]
                        dve.wait_ge(m_ps, n * NTASK + (t + 1))
                        dve.tensor_scalar(mrow[c][:, 0, :], src[0:GH * SUB, 0:P], -1.0, None, ALU.mult).then_inc(m_neg, 1)
                        dve.wait_ge(m_neg, n * HALF + (c + 1))
                        dve.scalar_tensor_tensor(mrow[c][:, 1, :], src[0:GH * SUB, 0:P], -1.0, mrow[c][:, 0, :],
                                                 ALU.mult, ALU.subtract).then_inc(m_read, 1)
                        return
                    c, h, i, k0, w, diagonal = x
                    at = h * SUB + i % SUB
                    to = mx[0][:, at:at + 1] if c == 0 else mxp[:, k0 // TB, at:at + 1]
                    dve.wait_ge(m_ps, n * NTASK + (t + 1))
                    dve.tensor_reduce(to, src[:, 0:w], AX.X, ALU.max).then_inc(m_read, 1)
                    if t + 1 == TURN[1]:
                        dve.wait_ge(m_read, n * NTASK + (t + 1 + PRE))
                        dve.tensor_tensor(mx[1][:, :], mxp[:, 0, :], mxp[:, 1, :], ALU.max).then_inc(mx_ready, 1)

                def invert(n, c, i):
                    if i == 0:
                        dve.wait_ge(acc_read, n * (2 * HALF) + (2 * c + 3))
                    part = rec[:, i * TB // PIECES:(i + 1) * TB // PIECES]
                    dve.reciprocal(part, part).then_inc(rec_ready, 1)

                def normalise(n, c):
                    dve.wait_ge(rec_ready, (n * HALF + (c + 1)) * PIECES)
                    dve.tensor_tensor(o32[c][:, :], o32[c][:, :], rec[:, :], ALU.mult).then_inc(o_ready, 1)

                def step(n, last, first=False):
                    for k in range(NS):
                        todo = [] if last else beside[k]
                        for x in range(4):
                            for t in todo[len(todo) * x // 4:len(todo) * (x + 1) // 4]:
                                maximum(n + 1, t)
                            if k in (1, 2) and not first:
                                invert(n - 1, 1, (k - 1) * 4 + x)
                            if k in (SUB + 1, SUB + 2):
                                invert(n, 0, (k - SUB - 1) * 4 + x)
                        if k == 2 and not first:
                            normalise(n - 1, 1)
                        if k == SUB + 2:
                            normalise(n, 0)

                for t in range(NTASK):
                    maximum(0, t)
                step(0, False, True)
                with dve.Fori(1, N - 1) as n:
                    step(n, False)
                step(N - 1, True)
                for i in range(PIECES):
                    invert(N - 1, 1, i)
                normalise(N - 1, 1)


class Routing:

    def __init__(self, ctx, nc):
        def sb(name, shape, dt):
            return ctx.enter_context(nc.sbuf_tensor(name, shape, dt))

        self.logits = sb("logits", [P, NT, NR], fp32)
        self.slots = sb("slots", [P, TOPK, NT], u32)
        self.weights = sb("weights", [P, TOPK, NT], fp32)
        self.shared = sb("shared_w", [P, NT], fp32)
        self.expert_at = sb("expert_at", [1, NX], i32)


def project_and_route(nc, a, s, ro):
    V = 4
    PAIRS = NT // 2
    with ExitStack() as ctx:
        def sb(name, shape, dt):
            return ctx.enter_context(nc.sbuf_tensor(name, shape, dt))

        def sem(name):
            return ctx.enter_context(nc.semaphore(name))

        work = sb("work3", [P, 4, D], fp32)
        wst, zt, h2 = work, [work[:, v, :] for v in range(2)], [work[:, 2 + v, :] for v in range(2)]
        wo = sb("wo_split", [P, 2, KT, D], fp16)
        mod = sb("mod_bc", [P, B, 3, D], fp32)
        rw = sb("router_w", [P, KT, NR], fp32)
        ident = sb("ident3", [P, P], fp32)
        eps = sb("eps3", [P, 1], fp32)
        at = [sb(f"at{q}", [P, NKV, 2, 2 * P], fp16) for q in range(2)]
        xt = [sb(f"x3_{v}", [P, D], fp32) for v in range(V)]
        gated = [sb(f"gated{v}", [P, D], fp32) for v in range(2)]
        ht = [sb(f"ht_{v}", [P, KT, P], fp32) for v in range(2)]
        hs = [sb(f"hs_{v}", [P, KT, 2, P], fp16) for v in range(2)]
        st = [sb(f"st3_{v}", [P, 6], fp32) for v in range(2)]
        mv = sb("mv3", [P, 2, 2], fp32)
        tick = sb("tick3", [P, 1], fp32)
        sd = sb("sd3", [P, 2], fp32)
        rs = sb("rs3", [P, 2], fp32)
        lg = ro.logits
        pY = [ctx.enter_context(nc.psum_tensor(f"pY3_{v}", [P, D], fp32)) for v in range(V)]
        pT = [ctx.enter_context(nc.psum_tensor(f"pT3_{v}", [P, KT, P], fp32)) for v in range(2)]
        pL = [ctx.enter_context(nc.psum_tensor(f"pL3_{v}", [P, TB], fp32)) for v in range(2)]

        consts, wo_in, mod_in, rw_in, wo_high, wo_low = (sem(n) for n in (
            "consts3", "wo_in", "mod_in", "rw_in", "wo_high", "wo_low"))
        at_in = [sem(f"at_in{q}") for q in range(2)]
        x_in = [sem(f"x_in3_{v}") for v in range(V)]
        y_ps, y_gated, x1_ready, stats, aggr, sd_ready, rs_ready, z_ready = (sem(n + "3") for n in (
            "y_ps", "y_gated", "x1_ready", "stats", "aggr", "sd_ready", "rs_ready", "z_ready"))
        h2_step, h_turned, ht_ready, ht_high, ht_low, l_ps, l_read = (sem(n + "3") for n in (
            "h2_step", "h_turned", "ht_ready", "ht_high", "ht_low", "l_ps", "l_read"))
        x1_out = [sem(f"x1_out{v}") for v in range(V)]
        h2_out = [sem(f"h2_out{v}") for v in range(2)]
        hs_out = [sem(f"hs_out{v}") for v in range(2)]

        x_v = a["L0_attn_x"].rearrange("b (n p) d -> (b n) p d", p=P)
        TPB = S // P

        def load_attention(engine, pair, q):
            engine.dma_start(at[q][:, :, :, :].rearrange("p g h t -> p (g h) t"),
                             s.att.rearrange("b g h p t -> b p (g h) t")
                             [bass.ds(pair // (TPB // 2), 1), :, :, bass.ds(pair % (TPB // 2) * (2 * P), 2 * P)]
                             .rearrange("o p g t -> p (o g) t")).then_inc(at_in[q], 16)

        with nc.Block() as block:
            @block.sync
            def _(sp):
                def load_x(n, v):
                    sp.dma_start(xt[v][:, :], x_v[bass.ds(n, 1), :, :].rearrange("o p d -> p (o d)")).then_inc(x_in[v], 16)

                load_attention(sp, 0, 0)
                sp.dma_start(wst[:, :, :], a["L0_attn_Wo"].rearrange("(k p) d -> p k d", p=P)).then_inc(wo_in, 16)
                load_attention(sp, 1, 1)
                for i, j in enumerate((2, 3, 4)):
                    sp.dma_start(mod[:, 0, i, :], s.mod[0, j:j + 1, :].to_broadcast([P, D])).then_inc(mod_in, 16)
                for v in range(V):
                    load_x(v, v)
                for b in range(1, B):
                    for i, j in enumerate((2, 3, 4)):
                        sp.dma_start(mod[:, b, i, :], s.mod[b, j:j + 1, :].to_broadcast([P, D])).then_inc(mod_in, 16)
                for k in range(KT):
                    sp.dma_start(rw[:, k, 0:E], a["L0_ffn_router_w"][:, k * P:(k + 1) * P].rearrange("e p -> p e"),
                                 allow_slow_non_contiguous=True).then_inc(rw_in, 16)
                    sp.dma_start(rw[:, k, E:NR], a["L0_ffn_shared_gate_w"][k * P:(k + 1) * P].rearrange("(p o) -> p o", o=1))\
                      .then_inc(rw_in, 16)

                def step(i, last):
                    for q in range(V // 2):
                        for w in range(2):
                            v = 2 * q + w
                            sp.wait_ge(x1_ready, i * V + (v + 1))
                            sp.dma_start(s.x1[bass.ds(i * V + v, 1), :, :].rearrange("o p d -> p (o d)"), xt[v][:, :])\
                              .then_inc(x1_out[v], 16)
                        for w in range(2):
                            n = i * V + (2 * q + w)
                            sp.wait_ge(h2_step, n * 2 + 2)
                            sp.dma_start(s.h2[bass.ds(n, 1), :, :].rearrange("o p d -> p (o d)"), h2[w]).then_inc(h2_out[w], 16)
                        for w in range(2):
                            v = 2 * q + w
                            if not last:
                                sp.wait_ge(x1_out[v], i * 16 + 16)
                                load_x((i + 1) * V + v, v)
                        for w in range(2):
                            n = i * V + (2 * q + w)
                            sp.wait_ge(ht_low, n + 1)
                            sp.dma_start(s.h2T[bass.ds(n, 1), :, :, :, :].rearrange("o p k h t -> p (o k h t)"),
                                         hs[w][:, :, :, :].rearrange("p k h t -> p (k h t)")).then_inc(hs_out[w], 16)

                with sp.Fori(0, NT // V - 1) as i:
                    step(i, False)
                step(NT // V - 1, True)
                for v in range(V):
                    sp.wait_ge(x1_out[v], NT // V * 16)
                for w in range(2):
                    sp.wait_ge(h2_out[w], NT // 2 * 16)
                    sp.wait_ge(hs_out[w], NT // 2 * 16)

            @block.gpsimd
            def _(pool):
                pool.memset(ident[:, :], 0.0).then_inc(consts, 1)
                pool.memset(eps[:, :], EPS).then_inc(consts, 1)
                pool.wait_ge(consts, 2)
                pool.affine_select(out=ident[:, :], in_=ident[:, :], compare_op=ALU.not_equal, fill=1.0,
                                   base=0, pattern=[[-1, P]], channel_multiplier=1).then_inc(consts, 1)
                pool.wait_ge(mod_in, 3 * B * 16)
                with pool.Fori(0, PAIRS) as i:
                    for w in range(2):
                        n = i * 2 + w
                        b = n // TPB
                        pool.wait_ge(h2_out[w], i * 16)
                        pool.wait_ge(h_turned, i * 2)
                        pool.wait_ge(z_ready, n + 1)
                        pool.tensor_tensor(h2[w], zt[w], mod[:, bass.ds(b, 1), 2, :].rearrange("p o d -> p (o d)"),
                                           ALU.mult).then_inc(h2_step, 1)
                        pool.wait_ge(h2_step, n * 2 + 1)
                        pool.tensor_tensor(h2[w], h2[w], mod[:, bass.ds(b, 1), 1, :].rearrange("p o d -> p (o d)"),
                                           ALU.add).then_inc(h2_step, 1)

            @block.tensor
            def _(pe):
                def project(n, i, v):
                    if v % 2 == 0:
                        pe.wait_ge(at_in[v // 2], i * 16 + 16)
                    if not (isinstance(i, int) and i == 0):
                        pe.wait_ge(y_gated, n - (V - 1))
                    for g in range(KT):
                        for ah, wh in ((0, 0), (0, 1), (1, 0)):
                            mm = pe.matmul(pY[v][:, :], at[v // 2][:, g, ah, v % 2 * P:(v % 2 + 1) * P], wo[:, wh, g, :],
                                           start=g == 0 and (ah, wh) == (0, 0), stop=g == KT - 1 and ah == 1)
                    mm.then_inc(y_ps, 1)

                def turn(n, w):
                    pe.wait_ge(h2_step, n * 2 + 2)
                    pe.wait_ge(ht_high, (n // 2) * 2)
                    for k in range(KT):
                        mm = pe.transpose(pT[w][:, k, :], h2[w][:, k * P:(k + 1) * P], ident[:, :])
                    mm.then_inc(h_turned, 1)

                def route(n, w):
                    pe.wait_ge(ht_ready, n + 1)
                    pe.wait_ge(l_read, (n // 2) * 2)
                    for k in range(KT):
                        mm = pe.matmul(pL[w][:, 0:NR], ht[w][:, k, :], rw[:, k, :], start=k == 0, stop=k == KT - 1)
                    mm.then_inc(l_ps, 1)

                def step(i, last):
                    for p in range(V // 2):
                        for v in (2 * p, 2 * p + 1):
                            turn(i * V + v, v % 2)
                        for v in (2 * p, 2 * p + 1):
                            if not last:
                                project((i + 1) * V + v, i + 1, v)
                        for v in (2 * p, 2 * p + 1):
                            route(i * V + v, v % 2)

                pe.wait_ge(wo_low, 1)
                for v in range(V):
                    project(v, 0, v)
                pe.wait_ge(consts, 3)
                pe.wait_ge(rw_in, 2 * KT * 16)
                with pe.Fori(0, NT // V - 1) as i:
                    step(i, False)
                step(NT // V - 1, True)

            @block.scalar
            def _(act):
                act.wait_ge(wo_in, 16)
                act.activation(wo[:, 0, :, :], wst[:, :, :], ACT.Copy, scale=WS).then_inc(wo_high, 1)
                act.wait_ge(consts, 3)

                def deviation(i):
                    act.wait_ge(aggr, i + 1)
                    act.activation(sd[:, :], mv[:, :, 1], ACT.Sqrt, bias=eps[:, :]).then_inc(sd_ready, 1)

                def pair(i, q, left):
                    for w in range(2):
                        n = i * 2 + w
                        act.wait_ge(h_turned, n + 1)
                        act.wait_ge(ht_low, i * 2)
                        act.wait_ge(l_ps, i * 2)
                        act.activation(ht[w][:, :, :], pT[w][:, :, :], ACT.Copy).then_inc(ht_ready, 1)
                        act.wait_ge(hs_out[w], i * 16)
                        act.activation(hs[w][:, :, 0, :], pT[w][:, :, :], ACT.Copy).then_inc(ht_high, 1)
                    for w in range(2):
                        n = i * 2 + w
                        act.wait_ge(l_ps, n + 1)
                        act.activation(lg[:, bass.ds(n, 1), :].rearrange("p o r -> p (o r)"), pL[w][:, 0:NR], ACT.Copy)\
                           .then_inc(l_read, 1)
                    if left > 3:
                        load_attention(act, i + 4, q)
                    if left > 1:
                        deviation(i + 2)

                deviation(0)
                deviation(1)
                act.wait_ge(y_ps, V)
                for q in range(2):
                    load_attention(act, q + 2, q)
                with act.Fori(0, PAIRS // 2 - 2) as j:
                    for q in range(2):
                        pair(j * 2 + q, q, 4)
                for i in range(PAIRS - 4, PAIRS):
                    pair(i, i % 2, PAIRS - i - 1)

            @block.vector
            def _(dve):
                dve.wait_ge(wo_high, 1)
                dve.scalar_tensor_tensor(wo[:, 1, :, :], wst[:, :, :], WS, wo[:, 0, :, :], ALU.mult, ALU.subtract)\
                   .then_inc(wo_low, 1)
                dve.wait_ge(mod_in, 3 * B * 16)
                dve.wait_ge(consts, 2)

                def norm(i, pair, q):
                    tiles = [(pair * 2 + w, 2 * q + w, w) for w in range(2)]
                    for n, v, w in tiles:
                        dve.wait_ge(y_ps, n + 1)
                        dve.scalar_tensor_tensor(gated[w][:, :], pY[v][:, :], 1 / WS,
                                                 mod[:, bass.ds(n // TPB, 1), 0, :].rearrange("p o d -> p (o d)"),
                                                 ALU.mult, ALU.mult).then_inc(y_gated, 1)
                    for n, v, w in tiles:
                        dve.wait_ge(x_in[v], i * 16 + 16)
                        dve.wait_ge(y_gated, n + 1)
                        dve.tensor_tensor(xt[v][:, :], gated[w][:, :], xt[v][:, :], ALU.add).then_inc(x1_ready, 1)
                    for n, v, w in tiles:
                        dve.wait_ge(x1_ready, n + 1)
                        dve.bn_stats(st[w][:, :], xt[v][:, :]).then_inc(stats, 1)
                    dve.wait_ge(stats, pair * 2 + 2)
                    dve.tensor_copy(tick[:, :], eps[:, :])
                    for w in range(2):
                        op = dve.bn_aggr(mv[:, w, :], st[w][:, :])
                    op.then_inc(aggr, 1)
                    dve.wait_ge(sd_ready, pair + 1)
                    dve.reciprocal(rs[:, :], sd[:, :]).then_inc(rs_ready, 1)
                    dve.wait_ge(rs_ready, pair + 1)
                    for n, v, w in tiles:
                        dve.wait_ge(h2_step, pair * 4)
                        dve.tensor_scalar(zt[w], xt[v][:, :], mv[:, w, 0:1], rs[:, w:w + 1],
                                          ALU.subtract, ALU.mult).then_inc(z_ready, 1)

                def low(pair):
                    for w in range(2):
                        dve.wait_ge(ht_high, pair * 2 + (w + 1))
                        dve.tensor_tensor(hs[w][:, :, 1, :], ht[w][:, :, :], hs[w][:, :, 0, :], ALU.subtract).then_inc(ht_low, 1)

                for q in range(2):
                    norm(0, q, q)
                with dve.Fori(0, PAIRS // 2 - 1) as i:
                    for q in range(2):
                        low(i * 2 + q)
                        norm(i + 1, i * 2 + (q + 2), q)
                for q in range(2):
                    low(PAIRS - 2 + q)


def choose(nc, ro):
    with ExitStack() as ctx:
        def sb(name, shape, dt):
            return ctx.enter_context(nc.sbuf_tensor(name, shape, dt))

        def sem(name):
            return ctx.enter_context(nc.semaphore(name))

        lg = ro.logits
        top = sb("top", [P, NT, 8], fp32)
        top_at = sb("top_at", [P, NT, 8], u32)
        choice = sb("choice", [P, TOPK, NT], fp32)
        iota_e = sb("iota_e", [P, E], fp32)
        iota_j = sb("iota_j", [P, NX], fp32)
        one_hot = [sb(f"one_hot{c}", [P, NT, E], fp32) for c in range(TOPK)]
        chosen = sb("chosen", [P, NT, E], bf16)
        before = sb("before", [P, P], bf16)
        ones = sb("ones4", [P, P], bf16)
        scan = [sb(f"scan{x}", [P, NT, E], fp32) for x in range(2)]
        total = sb("total", [P, NT, E], fp32)
        place = sb("place", [P, NT, E], fp32)
        part = sb("part", [P, NT, E], fp32)
        slot = sb("slot", [P, TOPK, NT], fp32)
        count = sb("count", [P, E], fp32)
        count_i = sb("count_i", [P, E], i32)
        tiles = sb("tiles", [P, E], fp32)
        end = [sb(f"end{x}", [P, E], fp32) for x in range(2)]
        after = sb("after", [P, NX, E], fp32)
        tile_e = sb("tile_e", [P, NX], fp32)
        diff = sb("diff", [P, NT], fp32)
        low = sb("low_w", [P, NT], fp32)
        gate = sb("gate_w", [P, NT], fp32)
        pC = ctx.enter_context(nc.psum_tensor("pC", [P, NT * E], fp32))
        pN = ctx.enter_context(nc.psum_tensor("pN", [P, NT * E], fp32))
        ready, consts, exps, step, counted = sem("chosen_ready"), sem("consts4"), sem("exps4"), sem("step4"), sem("counted")

        with nc.Block() as block:
            @block.gpsimd
            def _(pool):
                pool.iota(iota_e[:, :], pattern=[[1, E]], base=0, channel_multiplier=0,
                          allow_small_or_imprecise_dtypes=True).then_inc(consts, 1)
                pool.iota(iota_j[:, :], pattern=[[1, NX]], base=0, channel_multiplier=0,
                          allow_small_or_imprecise_dtypes=True).then_inc(consts, 1)
                pool.memset(ones[:, :], 1.0).then_inc(consts, 1)
                pool.wait_ge(consts, 3)
                pool.affine_select(out=before[:, :], in_=ones[:, :], compare_op=ALU.is_gt, fill=0.0,
                                   base=0, pattern=[[1, P]], channel_multiplier=-1).then_inc(consts, 1)

            @block.tensor
            def _(pe):
                pe.wait_ge(consts, 4)
                pe.wait_ge(ready, 1)
                flat = chosen[:, :, :].rearrange("p t e -> p (t e)")
                pe.matmul(pC[:, :], before[:, :], flat, start=True, stop=True).then_inc(counted, 1)
                pe.matmul(pN[:, :], ones[:, :], flat, start=True, stop=True).then_inc(counted, 1)

            @block.scalar
            def _(act):
                act.wait_ge(exps, 1)
                act.activation(low[:, :], diff[:, :], ACT.Exp).then_inc(exps, 1)
                act.activation(gate[:, :], lg[:, :, E], ACT.Exp, scale=-1.0).then_inc(exps, 1)

            @block.vector
            def _(dve):
                done = [0]

                def link(op):
                    done[0] += 1
                    op.then_inc(step, 1)
                    dve.wait_ge(step, done[0])

                for t in range(NT):
                    op = dve.max(top[:, t, :], lg[:, t, 0:E])
                link(op)
                for t in range(NT):
                    op = dve.max_index(top_at[:, t, :], top[:, t, :], lg[:, t, 0:E])
                link(op)
                dve.tensor_tensor(diff[:, :], top[:, :, 1], top[:, :, 0], ALU.subtract).then_inc(exps, 1)
                link(dve.tensor_copy(choice[:, :, :], top_at[:, :, 0:TOPK].rearrange("p t c -> p c t")))
                dve.wait_ge(consts, 4)
                for c in range(TOPK):
                    op = dve.tensor_tensor(one_hot[c][:, :, :], choice[:, c, :].rearrange("p (t o) -> p t o", o=1).to_broadcast([P, NT, E]),
                                           iota_e[:, :].rearrange("p (o e) -> p o e", o=1).to_broadcast([P, NT, E]), ALU.is_equal)
                link(op)
                dve.tensor_tensor(chosen[:, :, :], one_hot[0][:, :, :], one_hot[1][:, :, :], ALU.add).then_inc(ready, 1)
                dve.wait_ge(exps, 3)
                link(dve.tensor_scalar(diff[:, :], low[:, :], 1.0, None, ALU.add))
                link(dve.reciprocal(ro.weights[:, 0, :], diff[:, :]))
                dve.tensor_tensor(ro.weights[:, 1, :], ro.weights[:, 0, :], low[:, :], ALU.mult)
                link(dve.tensor_scalar(gate[:, :], gate[:, :], 1.0, None, ALU.add))
                link(dve.reciprocal(diff[:, :], gate[:, :]))
                dve.tensor_scalar(ro.shared[:, :], diff[:, :], 1 / WS, None, ALU.mult)
                dve.wait_ge(counted, 2)
                pn, pc = (x[:, :].rearrange("p (t e) -> p t e", e=E) for x in (pN, pC))
                dve.tensor_copy(total[:, :, :], pn)
                link(dve.tensor_copy(scan[0][:, :, :], pn))
                x, d = 0, 1
                while d < NT:
                    dve.tensor_copy(scan[1 - x][:, 0:d, :], scan[x][:, 0:d, :])
                    link(dve.tensor_tensor(scan[1 - x][:, d:, :], scan[x][:, d:, :], scan[x][:, 0:NT - d, :], ALU.add))
                    x, d = 1 - x, 2 * d
                link(dve.tensor_scalar(count[:, :], scan[x][:, NT - 1, :], float(P - 1), None, ALU.add))
                link(dve.tensor_copy(count_i[:, :], count[:, :]))
                link(dve.tensor_single_scalar(count_i[:, :], count_i[:, :], P.bit_length() - 1, ALU.arith_shift_right))
                link(dve.tensor_copy(tiles[:, :], count_i[:, :]))
                link(dve.tensor_copy(end[0][:, :], tiles[:, :]))
                y, d = 0, 1
                while d < E:
                    dve.tensor_copy(end[1 - y][:, 0:d], end[y][:, 0:d])
                    link(dve.tensor_tensor(end[1 - y][:, d:], end[y][:, d:], end[y][:, 0:E - d], ALU.add))
                    y, d = 1 - y, 2 * d
                link(dve.tensor_tensor(tiles[:, :], end[y][:, :], tiles[:, :], ALU.subtract))
                link(dve.tensor_scalar(tiles[:, :], tiles[:, :], float(P), None, ALU.mult))
                link(dve.tensor_tensor(place[:, :, :], scan[x][:, :, :], total[:, :, :], ALU.subtract))
                link(dve.tensor_tensor(place[:, :, :], place[:, :, :], pc, ALU.add))
                link(dve.tensor_tensor(place[:, :, :], place[:, :, :],
                                       tiles[:, :].rearrange("p (o e) -> p o e", o=1).to_broadcast([P, NT, E]), ALU.add))
                for c in range(TOPK):
                    link(dve.tensor_tensor(part[:, :, :], place[:, :, :], one_hot[c][:, :, :], ALU.mult))
                    link(dve.tensor_reduce(slot[:, c, :], part[:, :, :], AX.X, ALU.add))
                dve.tensor_copy(ro.slots[:, :, :], slot[:, :, :])
                link(dve.tensor_tensor(after[:, :, :], end[y][:, :].rearrange("p (o e) -> p o e", o=1).to_broadcast([P, NX, E]),
                                       iota_j[:, :].rearrange("p (j o) -> p j o", o=1).to_broadcast([P, NX, E]), ALU.is_le))
                link(dve.tensor_reduce(tile_e[:, :], after[:, :, :], AX.X, ALU.add))
                link(dve.tensor_scalar(tile_e[:, :], tile_e[:, :], float(E - 1), None, ALU.min))
                link(dve.tensor_copy(ro.expert_at[:, :], tile_e[0:1, :]))


def routed_experts(nc, s, ro, rw):
    RING = 4
    with ExitStack() as ctx:
        def sb(name, shape, dt):
            return ctx.enter_context(nc.sbuf_tensor(name, shape, dt))

        def sem(name):
            return ctx.enter_context(nc.semaphore(name))

        hr = [sb(f"hr{v}", [P, D], fp32) for v in range(RING)]
        ident = sb("ident5", [P, P], fp32)
        zero = sb("zero5", [P, P], fp32)
        xs = [sb(f"xs{u}", [P, D], fp32) for u in range(2)]
        xT = sb("xT5", [P, KT, 2, P], fp16)
        th = sb("th5", [P, I], fp32)
        gt = sb("gt5", [P, I], fp32)
        hb = sb("hb5", [P, IT * P], fp32)
        hT = sb("hT5", [P, IT, 2, P], fp16)
        ysb = [sb(f"ysb{u}", [P, D], fp32) for u in range(2)]
        pG = [ctx.enter_context(nc.psum_tensor(f"pG5_{w}", [P, I], fp32)) for w in range(2)]
        pX = ctx.enter_context(nc.psum_tensor("pX5", [P, KT, P], fp32))
        pH = ctx.enter_context(nc.psum_tensor("pH5", [P, IT, P], fp32))
        pY = [ctx.enter_context(nc.psum_tensor(f"pY5_{u}", [P, D], fp32)) for u in range(2)]

        hr_in = [sem(f"hr_in{v}") for v in range(RING)]
        hr_out = [sem(f"hr_out{v}") for v in range(RING)]
        consts, clear = sem("consts5"), sem("clear5")
        xs_in = [sem("xs_in0"), sem("xs_in1")]
        x_turned, x_high, x_low = sem("x_turned"), sem("x_high5"), sem("x_low5")
        gu_ps, th_ready, gt_ready, hb_ready = sem("gu_ps"), sem("th_ready"), sem("gt_ready"), sem("hb_ready")
        h_turned, h_high, h_low = sem("h_turned5"), sem("h_high5"), sem("h_low5")
        y_ps, y_read, y_out = sem("y_ps5"), sem("y_read5"), [sem("y_out0"), sem("y_out1")]
        rgu, rdn = routed_layout(rw)
        ys_v = s.ys.rearrange("(j p) d -> j p d", p=P)
        xs_flat = s.xs.rearrange("j p d -> (j p) d")

        with nc.Block() as block:
            @block.sync
            def _(sp):
                for v in range(RING):
                    sp.dma_start(hr[v][:, :], s.h2[v, :, :]).then_inc(hr_in[v], 16)
                with sp.Fori(0, NT // RING - 1) as i:
                    for v in range(RING):
                        sp.wait_ge(hr_out[v], (i + 1) * (TOPK * 16))
                        sp.dma_start(hr[v][:, :], s.h2[bass.ds((i + 1) * RING + v, 1), :, :]
                                     .rearrange("o p d -> p (o d)")).then_inc(hr_in[v], 16)
                for v in range(RING):
                    sp.wait_ge(hr_out[v], NT // RING * TOPK * 16)

                def load(j, u):
                    sp.dma_start(xs[u][:, :], s.xs[bass.ds(j, 1), :, :].rearrange("o p d -> p (o d)")).then_inc(xs_in[u], 16)

                def store(j, u):
                    sp.wait_ge(y_read, j + 3)
                    sp.dma_start(ys_v[bass.ds(j, 1), :, :].rearrange("o p d -> p (o d)"), ysb[u][:, :]).then_inc(y_out[u], 16)

                for u in range(2):
                    load(u, u)
                with sp.Fori(0, NX // 2 - 1) as i:
                    for u in range(2):
                        sp.wait_ge(x_turned, i * 2 + (u + 1))
                        load(i * 2 + (u + 2), u)
                        store(i * 2 + u, u)
                sp.wait_ge(x_turned, NX - 2)
                load(NX - 1, 0)
                for j in range(NX - 3, NX):
                    store(j, j % 2)
                for u in range(2):
                    sp.wait_ge(y_out[u], (NX + 1 - u) // 2 * 16)

            @block.gpsimd
            def _(pool):
                pool.memset(zero[:, :], 0.0).then_inc(consts, 1)
                pool.wait_ge(consts, 1)
                pool.affine_select(out=ident[:, :], in_=zero[:, :], compare_op=ALU.not_equal, fill=1.0,
                                   base=0, pattern=[[-1, P]], channel_multiplier=1).then_inc(consts, 1)
                for n in range(NT):
                    v = n % RING
                    pool.wait_ge(hr_in[v], (n // RING + 1) * 16)
                    for c in range(TOPK):
                        pool.indirect_dma_start(out=xs_flat, out_offset=bass.IndirectOffsetOnAxis(ap=ro.slots[:, c, n:n + 1], axis=0),
                                                in_=hr[v][:, :], in_offset=None).then_inc(hr_out[v], 16)

            @block.tensor
            def _(pe):
                def turn_x(j, u):
                    pe.wait_ge(xs_in[u], (j - u) * 8 + 16)
                    pe.wait_ge(x_low, j)
                    for k in range(KT):
                        mm = pe.transpose(pX[:, k, :], xs[u][:, k * P:(k + 1) * P], ident[:, :])
                    mm.then_inc(x_turned, 1)

                def gate_up(j, e):
                    pe.wait_ge(x_low, j + 1)
                    pe.wait_ge(hb_ready, j)
                    for k in range(KT):
                        for xh, wh in ((0, 0), (0, 1), (1, 0)):
                            for w in range(2):
                                mm = pe.matmul(pG[w][:, :], xT[:, k, xh, :],
                                               rgu[:, bass.ds(e, 1), k, wh, w, :].rearrange("p o i -> p (o i)"),
                                               start=k == 0 and (xh, wh) == (0, 0), stop=k == KT - 1 and xh == 1)
                    mm.then_inc(gu_ps, 1)

                def turn_h(j):
                    pe.wait_ge(hb_ready, j + 1)
                    pe.wait_ge(h_low, j)
                    for k in range(IT):
                        mm = pe.transpose(pH[:, k, :], hb[:, k * P:(k + 1) * P], ident[:, :])
                    mm.then_inc(h_turned, 1)

                def down(j, u, e):
                    pe.wait_ge(h_low, j + 1)
                    pe.wait_ge(y_read, j + 1)
                    for k in range(IT):
                        rows = P if k < IT - 1 else IR
                        for hh, wh in ((0, 0), (0, 1), (1, 0)):
                            mm = pe.matmul(pY[u][:, :], hT[0:rows, k, hh, :],
                                           rdn[0:rows, bass.ds(e, 1), k, wh, :].rearrange("p o d -> p (o d)"),
                                           start=k == 0 and (hh, wh) == (0, 0), stop=k == IT - 1 and hh == 1)
                    mm.then_inc(y_ps, 1)

                def expert(j):
                    return pe.value_load(ro.expert_at[0:1, bass.ds(j, 1)], min_val=0, max_val=E - 1)

                def tile(j, u, last):
                    e, e_last = expert(j), expert(j - 1)
                    gate_up(j, e)
                    down(j - 1, 1 - u, e_last)
                    if not last:
                        turn_x(j + 1, 1 - u)
                    turn_h(j)

                pe.wait_ge(consts, 2)
                turn_x(0, 0)
                gate_up(0, expert(0))
                turn_x(1, 1)
                turn_h(0)
                with pe.Fori(0, (NX - 3) // 2) as i:
                    tile(i * 2 + 1, 1, False)
                    tile(i * 2 + 2, 0, False)
                tile(NX - 2, 1, False)
                tile(NX - 1, 0, True)
                down(NX - 1, 0, expert(NX - 1))

            @block.scalar
            def _(act):
                def sigmoid_part(j):
                    act.wait_ge(gu_ps, j + 1)
                    act.activation(th[:, :], pG[0][:, :], ACT.Tanh, scale=0.5 / WS).then_inc(th_ready, 1)

                def high_x(j):
                    act.wait_ge(x_turned, j + 1)
                    act.activation(xT[:, :, 0, :], pX[:, :, :], ACT.Copy).then_inc(x_high, 1)

                def high_h(j):
                    act.wait_ge(h_turned, j + 1)
                    act.activation(hT[:, :, 0, :], pH[:, :, :], ACT.Copy).then_inc(h_high, 1)

                def result(j, u, stored):
                    act.wait_ge(y_out[u], stored * 16)
                    act.wait_ge(y_ps, j + 1)
                    act.activation(ysb[u][:, :], pY[u][:, :], ACT.Copy, scale=1 / WS).then_inc(y_read, 1)

                def tile(j, u, stored, last):
                    sigmoid_part(j)
                    result(j - 1, 1 - u, stored)
                    if not last:
                        high_x(j + 1)
                    high_h(j)

                high_x(0)
                sigmoid_part(0)
                high_x(1)
                high_h(0)
                with act.Fori(0, (NX - 3) // 2) as i:
                    tile(i * 2 + 1, 1, i, False)
                    tile(i * 2 + 2, 0, i, False)
                tile(NX - 2, 1, (NX - 3) // 2, False)
                tile(NX - 1, 0, (NX - 3) // 2, True)
                result(NX - 1, 0, (NX - 1) // 2)

            @block.vector
            def _(dve):
                dve.memset(hb[:, I:], 0.0)
                dve.memset(th[:, 0:1], 0.0).then_inc(y_read, 2)

                def mix(j):
                    dve.wait_ge(th_ready, j + 1)
                    dve.scalar_tensor_tensor(gt[:, :], th[:, :], 1.0, pG[0][:, :], ALU.add, ALU.mult).then_inc(gt_ready, 1)
                    dve.wait_ge(gt_ready, j + 1)
                    dve.scalar_tensor_tensor(hb[:, 0:I], gt[:, :], 0.5 / (WS * WS), pG[1][:, :], ALU.mult, ALU.mult)\
                       .then_inc(hb_ready, 1)

                def low_x(j):
                    dve.wait_ge(x_high, j + 1)
                    dve.tensor_tensor(xT[:, :, 1, :], pX[:, :, :], xT[:, :, 0, :], ALU.subtract).then_inc(x_low, 1)

                def low_h(j):
                    dve.wait_ge(h_high, j + 1)
                    dve.tensor_tensor(hT[:, :, 1, :], pH[:, :, :], hT[:, :, 0, :], ALU.subtract).then_inc(h_low, 1)

                def tile(j, last):
                    mix(j)
                    if not last:
                        low_x(j + 1)
                    low_h(j)

                low_x(0)
                mix(0)
                low_x(1)
                low_h(0)
                with dve.Fori(1, NX - 1) as j:
                    tile(j, False)
                tile(NX - 1, True)


def shared_expert_and_sum(nc, a, s, ro, out):
    with ExitStack() as ctx:
        def sb(name, shape, dt):
            return ctx.enter_context(nc.sbuf_tensor(name, shape, dt))

        def sem(name):
            return ctx.enter_context(nc.semaphore(name))

        wgu = sb("wgu6", [P, KT, 2, 2, SI], fp16)
        wdn = sb("wdn6", [P, ST, 2, D], fp16)
        gb = sb("gb6", [P, B, D], fp32)
        hT = [sb(f"hT6_{u}", [P, SUB, KT, 2, P], fp16) for u in range(2)]
        th = [sb(f"th6_{u}", [P, TB], fp32) for u in range(2)]
        gt = [sb(f"gt6_{u}", [P, TB], fp32) for u in range(2)]
        hb = [sb(f"hb6_{u}", [P, TB], fp32) for u in range(2)]
        sT = sb("sT6", [P, ST, 2, TB], fp16)
        yg = sb("yg6", [P, SUB, TOPK, D], fp32)
        x1 = sb("x16", [P, SUB, D], fp32)
        rt = [sb(f"rt6_{u}", [P, SUB, D], fp32) for u in range(2)]
        pG = [[ctx.enter_context(nc.psum_tensor(f"pG6_{x}{w}", [P, TB], fp32)) for w in range(2)] for x in range(2)]
        pY = [ctx.enter_context(nc.psum_tensor(f"pY6_{i}", [P, D], fp32)) for i in range(SUB)]

        gu_in = [sem(f"gu_in6_{k}") for k in range(KT)]
        dn_in, gb_in, x1_in = sem("dn_in6"), sem("gb_in6"), sem("x1_in6")
        h_in = [sem("h_in6_0"), sem("h_in6_1")]
        gu_ps, th_ready, gt_ready, hb_ready, s_high, s_low = (sem(n + "6") for n in (
            "gu_ps", "th_ready", "gt_ready", "hb_ready", "s_high", "s_low"))
        y_ps, y_read, y_in, first_mix, mixed, fin = (sem(n + "6") for n in (
            "y_ps", "y_read", "y_in", "first_mix", "mixed", "fin"))
        stored = [sem("stored6_0"), sem("stored6_1")]
        out_v = out.rearrange("b (n s p) d -> (b n) p s d", s=SUB, p=P)
        MIX = ST // 2

        with nc.Block() as block:
            @block.sync
            def _(sp):
                def load_h(n, u):
                    sp.dma_start(hT[u][:, :, :, :, :].rearrange("p s k h t -> p s (k h t)"),
                                 s.h2T[bass.ds(n * SUB, SUB), :, :, :, :].rearrange("s p k h t -> p s (k h t)")).then_inc(h_in[u], 16)

                load_h(0, 0)
                for k in range(KT):
                    sp.dma_start(wgu[:, k, :, :, :], s.sgu[:, k, :, :, :]).then_inc(gu_in[k], 16)
                sp.dma_start(wdn[:, :, :, :], s.sdn[:, :, :, :]).then_inc(dn_in, 16)
                load_h(1, 1)
                for b in range(B):
                    sp.dma_start(gb[:, b, :], s.mod[b, 5:6, :].to_broadcast([P, D])).then_inc(gb_in, 16)

                def tile(n, u, last):
                    if not last:
                        sp.wait_ge(gu_ps, (n + 1) * ST)
                        load_h(n + 2, u)
                    sp.wait_ge(fin, n * SUB * 2)
                    sp.dma_start(x1[:, :, :], s.x1[bass.ds(n * SUB, SUB), :, :].rearrange("s p d -> p s d")).then_inc(x1_in, 16)
                    sp.wait_ge(fin, (n + 1) * SUB * 2)
                    sp.dma_start(out_v[bass.ds(n, 1), :, :, :].rearrange("o p s d -> p (o s) d"), rt[u][:, :, :])\
                      .then_inc(stored[u], 16)

                with sp.Fori(0, NTB // 2 - 1) as i:
                    for u in range(2):
                        tile(i * 2 + u, u, False)
                for u in range(2):
                    tile(NTB - 2 + u, u, True)
                for u in range(2):
                    sp.wait_ge(stored[u], NTB // 2 * 16)

            @block.gpsimd
            def _(pool):
                pool.wait_ge(gb_in, B * 16)
                for n in range(NTB):
                    u = n % 2
                    pool.wait_ge(first_mix, n * SUB * 2)
                    for i in range(SUB):
                        for c in range(TOPK):
                            pool.indirect_dma_start(
                                out=yg[:, i, c, :], out_offset=None, in_=s.ys[:, :],
                                in_offset=bass.IndirectOffsetOnAxis(ap=ro.slots[:, c, n * SUB + i:n * SUB + i + 1], axis=0)).then_inc(y_in, 16)
                    pool.wait_ge(x1_in, (n + 1) * 16)
                    for i in range(SUB):
                        pool.wait_ge(y_read, n * SUB + i + 1)
                        pool.tensor_tensor(rt[u][:, i, :], rt[u][:, i, :], gb[:, n * TB // S, :], ALU.mult).then_inc(fin, 1)
                        pool.wait_ge(fin, (n * SUB + i) * 2 + 1)
                        pool.tensor_tensor(rt[u][:, i, :], rt[u][:, i, :], x1[:, i, :], ALU.add).then_inc(fin, 1)

            @block.tensor
            def _(pe):
                def gate_up(n, u, i, first=False):
                    x = (u * ST + i) % 2
                    if i == 0:
                        pe.wait_ge(h_in[u], (n - u) * 8 + 16)
                    if not first:
                        pe.wait_ge(hb_ready, n * ST + (i - 1))
                    for k in range(KT):
                        if first:
                            pe.wait_ge(gu_in[k], 16)
                        for w in range(2):
                            for wh, hh in ((0, 0), (0, 1), (1, 0)):
                                mm = pe.matmul(pG[x][w][:, :], wgu[:, k, w, wh, i * P:(i + 1) * P],
                                               hT[u][:, :, k, hh, :], start=k == 0 and (wh, hh) == (0, 0),
                                               stop=k == KT - 1 and wh == 1)
                    mm.then_inc(gu_ps, 1)

                def down(n, i):
                    pe.wait_ge(s_low, n * ST + (i + 1))
                    if i == 0:
                        pe.wait_ge(y_read, n * SUB)
                    for t in range(SUB):
                        for sh, wh in ((0, 0), (0, 1), (1, 0)):
                            mm = pe.matmul(pY[t][:, :], sT[:, i, sh, t * P:(t + 1) * P], wdn[:, i, wh, :],
                                           start=i == 0 and (sh, wh) == (0, 0), stop=i == ST - 1 and sh == 1)
                    mm.then_inc(y_ps, 1)

                def tile(n, u, last):
                    for i in range(ST):
                        if i + 1 < ST:
                            gate_up(n, u, i + 1, isinstance(n, int) and n == 0 and i == 0)
                        elif not last:
                            gate_up(n + 1, 1 - u, 0)
                        down(n, i)

                gate_up(0, 0, 0, True)
                pe.wait_ge(dn_in, 16)
                with pe.Fori(0, NTB // 2 - 1) as i:
                    tile(i * 2, 0, False)
                    tile(i * 2 + 1, 1, False)
                tile(NTB - 2, 0, False)
                tile(NTB - 1, 1, True)

            @block.scalar
            def _(act):
                def part(n, u, i):
                    x = (u * ST + i) % 2
                    act.wait_ge(gu_ps, n * ST + (i + 1))
                    act.activation(th[x][:, :], pG[x][0][:, :], ACT.Tanh, scale=0.5 / WS).then_inc(th_ready, 1)
                    act.wait_ge(hb_ready, n * ST + (i + 1))
                    act.activation(sT[:, i, 0, :], hb[x][:, :], ACT.Copy).then_inc(s_high, 1)

                with act.Fori(0, NTB // 2) as j:
                    for u in range(2):
                        for i in range(ST):
                            part(j * 2 + u, u, i)

            @block.vector
            def _(dve):
                def part(n, u, i):
                    x = (u * ST + i) % 2
                    at = n * ST + (i + 1)
                    dve.wait_ge(th_ready, at)
                    dve.scalar_tensor_tensor(gt[x][:, :], th[x][:, :], 1.0, pG[x][0][:, :], ALU.add, ALU.mult).then_inc(gt_ready, 1)
                    dve.wait_ge(gt_ready, at)
                    dve.scalar_tensor_tensor(hb[x][:, :], gt[x][:, :], 0.5 / (WS * WS), pG[x][1][:, :], ALU.mult, ALU.mult)\
                       .then_inc(hb_ready, 1)
                    dve.wait_ge(s_high, at)
                    dve.tensor_tensor(sT[:, i, 1, :], hb[x][:, :], sT[:, i, 0, :], ALU.subtract).then_inc(s_low, 1)

                def weigh(n, u, pair):
                    dve.wait_ge(stored[u], pair * 16)
                    dve.wait_ge(y_in, (n + 1) * (SUB * TOPK * 16))
                    for i in range(SUB):
                        at = n * SUB + i
                        dve.tensor_scalar(rt[u][:, i, :], yg[:, i, 0, :], ro.weights[:, 0, bass.ds(at, 1)], None, ALU.mult)\
                           .then_inc(first_mix, 1)
                    for i in range(SUB):
                        at = n * SUB + i
                        if i == 0:
                            dve.wait_ge(first_mix, n * (2 * SUB) + SUB)
                        dve.scalar_tensor_tensor(rt[u][:, i, :], yg[:, i, 1, :], ro.weights[:, 1, bass.ds(at, 1)], rt[u][:, i, :],
                                                 ALU.mult, ALU.add).then_inc(first_mix, 1)

                def add_shared(n, u):
                    dve.wait_ge(y_ps, (n + 1) * ST)
                    dve.wait_ge(first_mix, (n + 1) * (2 * SUB))
                    for i in range(SUB):
                        dve.scalar_tensor_tensor(rt[u][:, i, :], pY[i][:, :], ro.shared[:, bass.ds(n * SUB + i, 1)], rt[u][:, i, :],
                                                 ALU.mult, ALU.add).then_inc(y_read, 1)

                def tile(n, u, pair, last):
                    for i in range(ST):
                        if i + 1 < ST:
                            part(n, u, i + 1)
                        elif not last:
                            part(n + 1, 1 - u, 0)
                        if i == MIX:
                            weigh(n, u, pair)
                    add_shared(n, u)

                part(0, 0, 0)
                with dve.Fori(0, NTB // 2 - 1) as j:
                    tile(j * 2, 0, j, False)
                    tile(j * 2 + 1, 1, j, False)
                tile(NTB - 2, 0, NTB // 2 - 1, False)
                tile(NTB - 1, 1, NTB // 2 - 1, True)


def adaln_block(nc, a, out):
    s = Scratch(nc)
    modulation_and_qkv(nc, a, s)
    with ExitStack() as ctx:
        ro = Routing(ctx, nc)
        with nc.sbuf_tensor("routed_w", [P, E, RWC], fp16) as rw:
            attention(nc, a, s, rw)
            project_and_route(nc, a, s, ro)
            choose(nc, ro)
            routed_experts(nc, s, ro, rw)
        shared_expert_and_sum(nc, a, s, ro, out)


_INS = ["L0_attn_x", "L0_attn_Wq", "L0_attn_Wk", "L0_attn_Wv", "L0_attn_Wo", "L0_ffn_router_w",
        "L0_ffn_w_gate", "L0_ffn_w_up", "L0_ffn_w_down", "L0_ffn_sw_gate", "L0_ffn_sw_up",
        "L0_ffn_sw_down", "L0_ffn_shared_gate_w", "L0_c", "L0_wmod"]


def kernel(**inputs):
    import numpy as np
    import concourse.bacc as bacc
    from concourse.bass_utils import run_bass_kernel_spmd

    nc = bacc.Bacc("TRN2", target_bir_lowering=False, num_devices=1)
    arrays, aps = {}, {}
    for name in _INS:
        arrays[name] = np.ascontiguousarray(inputs[name])
        aps[name] = nc.dram_tensor(name, arrays[name].shape, mybir.dt.from_np(arrays[name].dtype), kind="ExternalInput").ap()
    out = nc.dram_tensor("out", (B, S, D), fp32, kind="ExternalOutput").ap()
    adaln_block(nc, aps, out)
    r = run_bass_kernel_spmd(nc, [arrays], core_ids=[0])
    return r.results[0]["out"]
```

```python
import concourse.bass as bass
from concourse import mybir
from contextlib import ExitStack

fp32 = mybir.dt.float32
fp16 = mybir.dt.float16
bf16 = mybir.dt.bfloat16
i32 = mybir.dt.int32
u32 = mybir.dt.uint32
ALU = mybir.AluOpType
ACT = mybir.ActivationFunctionType
AX = mybir.AxisListType

B, S, D = 4, 1024, 512
T = B * S
P = 128
KT = D // P
NH, NKV, HD = 16, 4, 32
GH = NH // NKV
E, TOPK, I, SI = 8, 2, 352, 1408
TB = 512
NTB = T // TB
NT = T // P
SUB = TB // P
EPS = 1e-5
WS = 32.0
QKVN = D + 2 * NKV * HD


IT = (I + P - 1) // P
IR = I - (IT - 1) * P
ST = SI // P
RWC = KT * 2 * 2 * I + IT * 2 * D
NX = TOPK * T // P + E - 1
NR = E + 1
N_ATT = B * NKV
XS_EACH = -(-NX // N_ATT)
FIRST = 2


class Scratch:

    def __init__(self, nc):
        def dram(name, shape, dt):
            return nc.dram_tensor(name, shape, dt, kind="Internal").ap()

        self.mod = dram("mod_s", [B, 6, D], fp32)
        self.q = dram("q_s", [B, NKV, 2, P, S], fp16)
        self.k = dram("k_s", [2, B, P, S], fp16)
        self.v = dram("v_s", [B, NKV, S, HD], fp32)
        self.maxima = dram("max_s", [S // TB, 2, GH * SUB, P], fp16)
        self.xs = dram("xs_s", [N_ATT * XS_EACH, P, D], fp32)
        self.ys = dram("ys_s", [NX * P, D], fp32)
        self.x1 = dram("x1_s", [T // P, P, D], fp32)
        self.h2 = dram("h2_s", [T // P, P, D], fp32)
        self.h2T = dram("h2T_s", [T // P, P, KT, 2, P], fp16)
        self.att = dram("att_s", [B, NKV, 2, P, S], fp16)
        self.sgu = dram("sgu_s", [ST, P, KT, 2, 2, P], fp16)
        self.sdn = dram("sdn_s", [ST, P, 2, D], fp16)
        self.shy = dram("shy_s", [FIRST * SUB, P, D], fp32)


def modulation_and_qkv(nc, a, s):
    NO = 6
    STORES = 5 + NKV
    EXTRA = ST - NTB
    BANKS = 4
    with nc.cleanup_on_exit(), ExitStack() as ctx:
        def sb(name, shape, dt):
            return ctx.enter_context(nc.sbuf_tensor(name, shape, dt))

        def sem(name):
            return nc.alloc_semaphore(name)

        ident = sb("ident1", [P, P], fp32)
        zero = sb("zero1", [P, P], fp32)
        eps = sb("eps1", [P, 1], fp32)
        credit = sb("credit1", [1, 1], fp32)
        cT = sb("cT", [P, KT, B], fp32)
        cth = sb("cth", [P, KT, B], fp32)
        csil = sb("csil", [P, KT, B], fp32)
        wm = sb("wm", [P, KT, 6, D], fp32)
        mod = sb("mod", [B, 6, D], fp32)
        gate = sb("gate", [B, D], fp32)
        gabs = sb("gabs", [B, D], fp32)
        gsgn = sb("gsgn", [B, D], fp32)
        caT = sb("caT", [P, KT, B], fp32)
        saT = sb("saT", [P, KT, B], fp32)
        wst = sb("wst", [P, KT, QKVN], fp32)
        wsp = sb("wsp", [P, KT, 2, QKVN], fp16)
        xt = [sb(f"xt{u}", [P, SUB, D], fp32) for u in range(2)]
        st = sb("st", [P, SUB, 6], fp32)
        mv = sb("mv", [P, SUB, 2], fp32)
        sd = sb("sd", [P, SUB, 1], fp32)
        rs = sb("rs", [P, SUB, 1], fp32)
        zt = sb("zt", [P, SUB, D], fp32)
        h32 = sb("h32", [P, KT, TB], fp32)
        hT = [sb(f"hT{u}", [P, KT, 2, TB], fp16) for u in range(2)]
        qs = [sb(f"qs{u}", [P, 5, 2, TB], fp16) for u in range(2)]
        vs = [sb(f"vs{u}", [P, SUB, P], fp32) for u in range(2)]
        scale = sb("scale1", [P, 1], fp32)
        sws = sb("sws", [P, SI + D], fp32)
        swp = [sb(f"swp{x}", [P, 2, SI + D], fp16) for x in range(2)]
        pT = [ctx.enter_context(nc.psum_tensor(f"pT{k}", [P, TB], fp32)) for k in range(KT)]
        pO = [ctx.enter_context(nc.psum_tensor(f"pO{k}", [P, TB], fp32)) for k in range(BANKS)]

        c_in, wm_in, wq_in = sem("c_in"), [sem(f"wm_in{j}") for j in range(6)], sem("wq_in")
        ident_set, eps_set = sem("ident_set"), sem("eps_set")
        c_tanh, c_silu, gate_step = sem("c_tanh"), sem("c_silu"), sem("gate_step")
        mod_ps, mod_sb, mod_out, modT_in = sem("mod_ps"), sem("mod_sb"), sem("mod_out"), sem("modT_in")
        w_high, w_low = sem("w_high"), sem("w_low")
        x_in = [sem("x_in0"), sem("x_in1")]
        stats, aggr, sd_ready, rs_ready = sem("stats"), sem("aggr"), sem("sd_ready"), sem("rs_ready")
        z_ready, z_turned, h_ready = sem("z_ready"), sem("z_turned"), sem("h_ready")
        h_high, h_low = sem("h_high"), sem("h_low")
        o_ps, o_high, o_read = sem("o_ps"), sem("o_high"), sem("o_read")
        q_stored = [sem("q_stored0"), sem("q_stored1")]
        sw_in, sw_step, scale_set = sem("sw_in"), sem("sw_step"), sem("scale_set")
        sw_stored = [sem("sw_stored0"), sem("sw_stored1")]

        x_v = a["L0_attn_x"].rearrange("b (n s p) d -> (b n) p s d", s=SUB, p=P)
        with nc.Block() as block:
            @block.sync
            def _(sp):
                for k in range(KT):
                    sp.dma_start(cT[:, k, :], a["L0_c"][:, k * P:(k + 1) * P].rearrange("b p -> p b"),
                                 allow_slow_non_contiguous=True).then_inc(c_in, 16)
                wm_v = a["L0_wmod"].rearrange("(k p) (j d) -> p k j d", p=P, j=6)
                for j in range(2):
                    sp.dma_start(wm[:, :, j, :], wm_v[:, :, j, :]).then_inc(wm_in[j], 16)
                sp.dma_start(xt[0][:, :, :], x_v[0, :, :, :]).then_inc(x_in[0], 16)
                for w, at, n in (("Wq", 0, D), ("Wk", D, P), ("Wv", D + P, P)):
                    sp.dma_start(wst[:, :, at:at + n],
                                 a["L0_attn_" + w].rearrange("(k p) n -> p k n", p=P)).then_inc(wq_in, 16)

                def load_shared(n, k, w):
                    sp.dma_start(sws[:, 0:SI], a["L0_ffn_sw_" + ("gate", "up")[w]].rearrange("(k p) c -> p k c", p=P)
                                 [:, bass.ds(k, 1), :].rearrange("p k c -> p (k c)")).then_inc(sw_in, 16)
                    sp.dma_start(sws[:, SI:], sdn_v[:, bass.ds(n, 1), :].rearrange("p k c -> p (k c)")).then_inc(sw_in, 16)

                sdn_v = a["L0_ffn_sw_down"].rearrange("(k p) c -> p k c", p=P)
                sp.wait_ge(mod_sb, 2)
                sp.dma_start(s.mod[:, 0:2, :], mod[:, 0:2, :]).then_inc(mod_out, 16)
                sp.wait_ge(mod_out, 16)
                for k in range(KT):
                    for j, to in ((0, saT), (1, caT)):
                        sp.dma_start(to[:, k, :], s.mod[:, j, k * P:(k + 1) * P].rearrange("b p -> p b"),
                                     allow_slow_non_contiguous=True)\
                          .then_inc(modT_in, 16)

                sp.dma_start(xt[1][:, :, :], x_v[1, :, :, :]).then_inc(x_in[1], 16)
                sp.dma_start(sws[:, 0:EXTRA * D].rearrange("p (k c) -> p k c", k=EXTRA), sdn_v[:, NTB:, :]).then_inc(sw_in, 16)
                for j in range(2, 6):
                    sp.dma_start(wm[:, :, j, :], wm_v[:, :, j, :]).then_inc(wm_in[j], 16)
                sp.wait_ge(sw_step, 3)
                for hl in range(2):
                    sp.dma_start(s.sdn[NTB:, :, hl, :].rearrange("k p c -> p k c"),
                                 swp[0][:, hl, 0:EXTRA * D].rearrange("p (k c) -> p k c", k=EXTRA))\
                      .then_inc(sw_stored[0], 16)
                load_shared(0, 0, 0)

                def tiles(b, last):
                    for u in range(2):
                        n = b * 2 + u if last else sp.snap(b * 2 + u)
                        for r in range(NO):
                            if r == 3:
                                sp.wait_ge(sw_step, (n + 2) * 3)
                                if not (last and u == 1):
                                    load_shared(n + 1, b + u, 1 - u)
                                for hl in range(2):
                                    sp.dma_start(s.sgu[:, :, bass.ds(b, 1), u, hl, :].rearrange("i p o c -> p (i o) c"),
                                                 swp[1 - u][:, hl, 0:SI].rearrange("p (i c) -> p i c", c=P))\
                                      .then_inc(sw_stored[1 - u], 16)
                                sp.dma_start(s.sdn[bass.ds(n, 1), :, :, :].rearrange("o p h c -> p (o h) c"),
                                             swp[1 - u][:, :, SI:]).then_inc(sw_stored[1 - u], 16)
                            if r == NKV:
                                continue
                            sp.wait_ge(o_read, n * NO + (r + 1 + BANKS))
                            tok = slice(u * TB, (u + 1) * TB)
                            if r < NKV:
                                sp.dma_start(s.q[bass.ds(b, 1), r, :, :, tok].rearrange("o h p t -> p (o h) t"),
                                             qs[u][:, r, :, :]).then_inc(q_stored[u], 16)
                            else:
                                sp.dma_start(s.k[:, bass.ds(b, 1), :, tok].rearrange("h o p t -> p (o h) t"),
                                             qs[u][:, NKV, :, :]).then_inc(q_stored[u], 16)
                                for g in range(NKV):
                                    sp.dma_start(s.v[bass.ds(b, 1), g, tok, :].rearrange("o (s p) c -> p (o s) c", p=P),
                                                 vs[u][:, :, g * HD:(g + 1) * HD]).then_inc(q_stored[u], 16)

                with sp.Fori(0, B - 1) as b:
                    tiles(b, False)
                tiles(B - 1, True)
                sp.wait_ge(mod_sb, 6)
                sp.dma_start(s.mod[:, 2:6, :], mod[:, 2:6, :]).then_inc(mod_out, 16)
                sp.wait_ge(mod_out, 32)
                for x in range(2):
                    sp.wait_ge(sw_stored[x], NTB // 2 * 48 + 32 * (1 - x))
                for u in range(2):
                    sp.wait_ge(q_stored[u], B * STORES * 16)

            @block.gpsimd
            def _(pool):
                pool.memset(eps[:, :], EPS).then_inc(eps_set, 1)
                pool.memset(zero[:, :], 0.0).then_inc(ident_set, 1)
                pool.wait_ge(ident_set, 1)
                pool.affine_select(out=ident[:, :], in_=zero[:, :], compare_op=ALU.not_equal, fill=1.0,
                                   base=0, pattern=[[-1, P]], channel_multiplier=1).then_inc(ident_set, 1)
                pool.memset(scale[:, :], WS).then_inc(scale_set, 1)
                pool.wait_ge(scale_set, 1)

                def split_shared(j, x, width):
                    by = scale[:, :].to_broadcast([P, width])
                    pool.tensor_tensor(swp[x][:, 0, 0:width], sws[:, 0:width], by, ALU.mult).then_inc(sw_step, 1)
                    pool.wait_ge(sw_step, j * 3 + 1)
                    pool.tensor_tensor(sws[:, 0:width], sws[:, 0:width], by, ALU.mult).then_inc(sw_step, 1)
                    pool.wait_ge(sw_step, j * 3 + 2)
                    pool.tensor_tensor(swp[x][:, 1, 0:width], sws[:, 0:width], swp[x][:, 0, 0:width], ALU.subtract)\
                        .then_inc(sw_step, 1)

                pool.wait_ge(sw_in, 16)
                split_shared(0, 0, EXTRA * D)

                with pool.Fori(0, B) as b:
                    for u in range(2):
                        pool.wait_ge(sw_stored[1 - u], b * 48 + 32 * u)
                        pool.wait_ge(sw_in, (b * 2 + (u + 1)) * 32 + 16)
                        split_shared(b * 2 + (u + 1), 1 - u, SI + D)

            @block.tensor
            def _(pe):
                def modulation(jj):
                    for j in jj:
                        pe.wait_ge(wm_in[j], 16)
                        for k in range(KT):
                            mm = pe.matmul(pT[j % KT][0:B, :], csil[:, k, :], wm[:, k, j, :],
                                           start=k == 0, stop=k == KT - 1)
                        mm.then_inc(mod_ps, 1)

                def turn(n):
                    for i in range(SUB):
                        pe.wait_ge(z_ready, n * SUB + (i + 1))
                        for k in range(KT):
                            mm = pe.transpose(pT[k][:, i * P:(i + 1) * P], zt[:, i, k * P:(k + 1) * P],
                                              ident[:, :])
                        mm.then_inc(z_turned, 1)

                def result(n, u, r):
                    if r == 0:
                        pe.wait_ge(h_low, (n + 1) * KT)
                    pe.wait_ge(o_read, n * NO + (r + 1))
                    out = pO[(NO * u + r) % BANKS]
                    if r < 5:
                        for k in range(KT):
                            for wl, hl in ((0, 0), (0, 1), (1, 0)):
                                mm = pe.matmul(out[:, :], wsp[:, k, wl, r * P:(r + 1) * P], hT[u][:, k, hl, :],
                                               start=k == 0 and (wl, hl) == (0, 0),
                                               stop=k == KT - 1 and wl == 1)
                    else:
                        for i in range(SUB):
                            for k in range(KT):
                                for hl, wl in ((0, 0), (0, 1), (1, 0)):
                                    mm = pe.matmul(out[:, i * P:(i + 1) * P], hT[u][:, k, hl, i * P:(i + 1) * P],
                                                   wsp[:, k, wl, 5 * P:6 * P],
                                                   start=k == 0 and (hl, wl) == (0, 0),
                                                   stop=k == KT - 1 and hl == 1)
                    mm.then_inc(o_ps, 1)

                def tile(n, u, last):
                    for r in range(3):
                        result(n, u, r)
                    if not last:
                        turn(n + 1)
                    for r in range(3, NO):
                        result(n, u, r)

                pe.wait_ge(c_silu, 2)
                modulation((0, 1))
                pe.wait_ge(ident_set, 2)
                pe.wait_ge(mod_sb, 2)
                turn(0)
                pe.wait_ge(w_low, 1)
                with pe.Fori(0, B - 1) as b:
                    tile(b * 2, 0, False)
                    tile(b * 2 + 1, 1, False)
                tile(2 * B - 2, 0, False)
                tile(2 * B - 1, 1, True)
                modulation((2, 3, 4, 5))

            @block.scalar
            def _(act):
                act.wait_ge(c_in, KT * 16)
                act.activation(cth[:, :, :], cT[:, :, :], ACT.Tanh, scale=0.5).then_inc(c_tanh, 1)
                def deviation(n):
                    act.wait_ge(aggr, n + 1)
                    act.activation(sd[:, :, 0], mv[:, :, 1], ACT.Sqrt, bias=eps[:, :]).then_inc(sd_ready, 1)

                def high_parts(n, u):
                    for k in range(KT):
                        act.wait_ge(h_ready, n * KT + (k + 1))
                        act.activation(hT[u][:, k, 0, :], h32[:, k, :], ACT.Copy).then_inc(h_high, 1)

                def results(n, b, u, rr):
                    for r in rr:
                        act.wait_ge(o_ps, n * NO + (r + 1))
                        if r == 0:
                            act.wait_ge(q_stored[u], b * (STORES * 16))
                        act.activation(qs[u][:, r, 0, :], pO[(NO * u + r) % BANKS][:, :], ACT.Copy,
                                       scale=1 / WS).then_inc(o_high, 1)

                def tile(n, b, u, last, more=True):
                    if more:
                        act.wait_ge(z_ready, (n + 1) * SUB)
                        act.dma_start(xt[u][:, :, :], x_v[bass.ds(n + 2, 1), :, :, :]
                                      .rearrange("o p s d -> p (o s) d")).then_inc(x_in[u], 16)
                    if not last:
                        deviation(n + 1)
                    results(n, b, u, range(3))
                    if not last:
                        high_parts(n + 1, 1 - u)
                    results(n, b, u, range(3, 5))

                act.wait_ge(eps_set, 1)
                deviation(0)
                act.wait_ge(wq_in, 48)
                act.activation(wsp[:, :, 0, :], wst[:, :, :], ACT.Copy, scale=WS).then_inc(w_high, 1)
                high_parts(0, 0)
                with act.Fori(0, B - 1) as b:
                    tile(b * 2, b, 0, False)
                    tile(b * 2 + 1, b, 1, False)
                tile(2 * B - 2, B - 1, 0, False, False)
                tile(2 * B - 1, B - 1, 1, True, False)

            @block.vector
            def _(dve):
                dve.memset(credit[:, :], 0.0).then_inc(o_read, BANKS)
                dve.wait_ge(c_tanh, 1)
                dve.scalar_tensor_tensor(cth[:, :, :], cth[:, :, :], 1.0, cT[:, :, :], ALU.add, ALU.mult)\
                   .then_inc(c_silu, 1)
                dve.wait_ge(c_silu, 1)
                dve.tensor_scalar(csil[:, :, :], cth[:, :, :], 0.5, None, ALU.mult).then_inc(c_silu, 1)

                def normalise(n, b, u):
                    dve.wait_ge(x_in[u], (b + 1) * 16)
                    for i in range(SUB):
                        op = dve.bn_stats(st[:, i, :], xt[u][:, i, :])
                    op.then_inc(stats, 1)
                    dve.wait_ge(sd_ready, n)
                    dve.wait_ge(stats, n + 1)
                    for i in range(SUB):
                        if i == 0:
                            dve.tensor_copy(credit[:, :], credit[:, :])
                        op = dve.bn_aggr(mv[:, i, :], st[:, i, :])
                    op.then_inc(aggr, 1)
                    dve.wait_ge(sd_ready, n + 1)
                    dve.reciprocal(rs[:, :, :], sd[:, :, :]).then_inc(rs_ready, 1)
                    dve.wait_ge(rs_ready, n + 1)
                    for i in range(SUB):
                        dve.tensor_scalar(zt[:, i, :], xt[u][:, i, :], mv[:, i, 0:1], rs[:, i, 0:1],
                                          ALU.subtract, ALU.mult).then_inc(z_ready, 1)

                def modulate(n, b):
                    dve.wait_ge(z_turned, (n + 1) * SUB)
                    for k in range(KT):
                        dve.tensor_scalar(h32[:, k, :], pT[k][:, :], caT[:, k, bass.ds(b, 1)], saT[:, k, bass.ds(b, 1)],
                                          ALU.mult, ALU.add).then_inc(h_ready, 1)

                def low_parts(n, u):
                    for k in range(KT):
                        dve.wait_ge(h_high, n * KT + (k + 1))
                        dve.tensor_tensor(hT[u][:, k, 1, :], h32[:, k, :], hT[u][:, k, 0, :], ALU.subtract).then_inc(h_low, 1)

                def results(n, u, rr):
                    for r in rr:
                        out = pO[(NO * u + r) % BANKS]
                        if r < 5:
                            dve.wait_ge(o_high, n * 5 + (r + 1))
                            dve.scalar_tensor_tensor(qs[u][:, r, 1, :], out[:, :], 1 / WS, qs[u][:, r, 0, :],
                                                     ALU.mult, ALU.subtract).then_inc(o_read, 1)
                        else:
                            dve.wait_ge(o_ps, n * NO + (r + 1))
                            dve.tensor_scalar(vs[u][:, :, :], out[:, :].rearrange("p (s c) -> p s c", s=SUB),
                                              1 / WS, None, ALU.mult).then_inc(o_read, 1)

                def tile(n, b, u, last):
                    if not last:
                        normalise(n + 1, b + u, 1 - u)
                    results(n, u, range(3))
                    if not last:
                        modulate(n + 1, b + u)
                    results(n, u, range(3, 4))
                    if not last:
                        low_parts(n + 1, 1 - u)
                    results(n, u, range(4, NO))

                for j in range(2):
                    dve.wait_ge(mod_ps, j + 1)
                    dve.tensor_scalar(mod[:, j, :], pT[j][0:B, :], float(j), None, ALU.add).then_inc(mod_sb, 1)
                normalise(0, 0, 0)
                dve.wait_ge(w_high, 1)
                dve.scalar_tensor_tensor(wsp[:, :, 1, :], wst[:, :, :], WS, wsp[:, :, 0, :],
                                         ALU.mult, ALU.subtract).then_inc(w_low, 1)
                dve.wait_ge(modT_in, 2 * KT * 16)
                modulate(0, 0)
                low_parts(0, 0)
                with dve.Fori(0, B - 1) as b:
                    tile(b * 2, b, 0, False)
                    tile(b * 2 + 1, b, 1, False)
                tile(2 * B - 2, B - 1, 0, False)
                tile(2 * B - 1, B - 1, 1, True)
                for step, j in enumerate((2, 5)):
                    dve.wait_ge(mod_ps, j + 1)
                    dve.tensor_copy(gate[:, :], pT[j % KT][0:B, :]).then_inc(gate_step, 1)
                    dve.wait_ge(gate_step, 4 * step + 1)
                    dve.scalar_tensor_tensor(gabs[:, :], gate[:, :], -1.0, gate[:, :], ALU.mult, ALU.max)\
                       .then_inc(gate_step, 1)
                    dve.tensor_scalar(gsgn[:, :], gate[:, :], 0.0, 2.0, ALU.is_ge, ALU.mult).then_inc(gate_step, 1)
                    dve.wait_ge(gate_step, 4 * step + 3)
                    dve.tensor_scalar(gabs[:, :], gabs[:, :], 0.25, None, ALU.max).then_inc(gate_step, 1)
                    dve.wait_ge(gate_step, 4 * step + 4)
                    dve.scalar_tensor_tensor(mod[:, j, :], gsgn[:, :], -1.0, gabs[:, :], ALU.add, ALU.mult)\
                       .then_inc(mod_sb, 1)
                for j in (3, 4):
                    dve.tensor_scalar(mod[:, j, :], pT[j % KT][0:B, :], float(j - 3), None, ALU.add).then_inc(mod_sb, 1)


def routed_layout(rw):
    gu = KT * 2 * 2 * I
    return (rw[:, :, 0:gu].rearrange("p e (k h w i) -> p e k h w i", k=KT, h=2, w=2),
            rw[:, :, gu:].rearrange("p e (k h d) -> p e k h d", k=IT, h=2))


def attention(nc, a, s, rw):
    SCALE = HD ** -0.5
    NEG = -1e30
    HALF = S // TB
    KEYS = S // P
    ROWS = 3 * HD
    STEPS = [(c, j) for c in range(HALF) for j in range((c + 1) * SUB)]
    NS = len(STEPS)
    N = B * NKV
    PIECES = 8
    START = 2
    PRE = 2

    def cols(k):
        c, j = STEPS[k]
        off = max(0, j - c * SUB) * P
        return c, j, off, TB - off

    tasks = []
    for c in range(HALF):
        for i in range(c * SUB, (c + 1) * SUB):
            for h in range(GH):
                for k0 in range(0, (i + 1) * P, TB):
                    n = min(TB, (i + 1) * P - k0)
                    tasks.append((c, h, i, k0, n, k0 + n == (i + 1) * P))
        tasks.append((c,))
    NTASK = len(tasks)
    TURN = [t for t, x in enumerate(tasks) if len(x) == 1]
    order = [*range(START, NS), *range(START)]
    share = [(cols(k)[3] + 200) * (0.0 if k == 1 else 0.6 if k == 0 else 1) for k in order]
    cost = [x[4] + 130 if len(x) > 1 else 400 for x in tasks]
    beside, done = [[] for k in range(NS)], 0
    for x, k in enumerate(order):
        upto = sum(share[:x + 1]) / sum(share) * sum(cost)
        while done < NTASK and sum(cost[:done + 1]) <= upto + 1:
            beside[k].append(done)
            done += 1
    assert done == NTASK and TURN[0] < beside[0][0] <= TURN[1]

    def maxima(n, k, x, last):
        todo = [] if last and k >= START else beside[k]
        return [(n + 1 if k >= START else n, t) for t in todo[len(todo) * x // 4:len(todo) * (x + 1) // 4]]

    with ExitStack() as ctx:
        def sb(name, shape, dt):
            return ctx.enter_context(nc.sbuf_tensor(name, shape, dt))

        def sem(name):
            return ctx.enter_context(nc.semaphore(name))

        qst = [sb(f"qst{u}", [P, GH, S], fp16) for u in range(2)]
        kst = [sb(f"kst{u}", [P, S], fp16) for u in range(2)]
        vt = [sb(f"vt{u}", [P, KEYS, HD], fp32) for u in range(2)]
        pb = [sb(f"pb{u}", [P, GH, TB], fp32) for u in range(2)]
        rec = sb("rec", [P, TB], fp32)
        o32 = [sb(f"o32{c}", [P, TB], fp32) for c in range(HALF)]
        ohl = [sb(f"ohl{c}", [P, 2, TB], fp16) for c in range(HALF)]
        gust = sb("gust", [P, 2, KT, I], fp32)
        dnst = sb("dnst", [P, IT, D], fp32)
        ident = sb("ident2", [P, P], fp32)
        identb = sb("identb2", [P, P], bf16)
        mask_m = sb("mask_m", [P, P], bf16)
        mask_s = sb("mask_s", [P, P], bf16)
        zero = sb("zero2", [P, P], bf16)
        ones = sb("ones2", [P, HD], fp32)
        scale = sb("scale2", [P, 1], fp32)
        one = sb("one2", [P, 1], fp32)
        gate_op = sb("gate_op", [P, 1], fp32)
        clear = sb("clear", [P, P], fp32)
        mxp = sb("mxp", [P, 2, GH * SUB], fp32)
        mx = [sb(f"mx{c}", [P, GH * SUB], fp32) for c in range(HALF)]
        mrow = [sb(f"mrow{c}", [GH * SUB, 2, P], fp16) for c in range(HALF)]
        pS = [ctx.enter_context(nc.psum_tensor(f"pS{x}", [P, 2, TB], fp32)) for x in range(2)]
        pM = [ctx.enter_context(nc.psum_tensor(f"pM{x}", [P, TB], fp32)) for x in range(PRE)]
        pA = ctx.enter_context(nc.psum_tensor("pA", [P, TB], fp32))
        pD = ctx.enter_context(nc.psum_tensor("pD", [P, TB], fp32))

        consts = sem("consts2")
        qk_in, v_in = [sem("qk_in0"), sem("qk_in1")], [sem("v_in0"), sem("v_in1")]
        m_ps, m_read, m_neg, mx_ready = sem("m_ps"), sem("m_read"), sem("m_neg"), sem("mx_ready")
        max_out = sem("max_out")
        max_in = [sem(f"max_in{c}") for c in range(HALF)]
        s_ps, p_ready, p_free = sem("s_ps"), sem("p_ready"), sem("p_free")
        acc_read, rec_ready, o_ready, o_split = sem("acc_read"), sem("rec_ready"), sem("o_ready"), sem("o_split")
        att_out = [sem(f"att_out{c}") for c in range(HALF)]
        gu_in, dn_in, gu_step, dn_step = sem("gu_in"), sem("dn_in"), sem("gu_step"), sem("dn_step")
        clear_set, xs_clear = sem("clear_set"), sem("xs_clear")
        NCONST = 11
        LOADS = 6

        q_v = s.q.rearrange("b g h p t -> (b g) h p t")
        a_v = s.att.rearrange("b g h p t -> (b g) h p t")
        k_v = s.k.rearrange("h b (g p) t -> h (b g) p t", g=NKV)
        v_v = s.v.rearrange("b g (j p) c -> (b g) p j c", p=P)
        rgu, rdn = routed_layout(rw)

        with nc.Block() as block:
            @block.sync
            def _(sp):
                def load_qk(n, u):
                    for at, hl in ((0, 0), (1, 1), (2, 0)):
                        sp.dma_start(qst[u][at * HD:(at + 1) * HD, :, :],
                                     q_v[bass.ds(n, 1), hl, :, :].rearrange("o (h p) t -> p (o h) t", p=HD))\
                          .then_inc(qk_in[u], 16)
                    for at, hl in ((0, 0), (1, 0), (2, 1)):
                        sp.dma_start(kst[u][at * HD:(at + 1) * HD, :],
                                     k_v[hl, bass.ds(n, 1), :, :].rearrange("o p t -> p (o t)")).then_inc(qk_in[u], 16)

                def load_v(n, u):
                    for j in (KEYS // 2, 0):
                        sp.dma_start(vt[u][:, j:j + KEYS // 2, :], v_v[bass.ds(n, 1), :, j:j + KEYS // 2, :]
                                     .rearrange("o p j c -> p (o j) c")).then_inc(v_in[u], 16)

                def load_gate_up(e):
                    for w, name in enumerate(("w_gate", "w_up")):
                        sp.dma_start(gust[:, w, :, :], a["L0_ffn_" + name][bass.ds(e, 1), :, :]
                                     .rearrange("o (k p) i -> p (o k) i", p=P)).then_inc(gu_in, 16)

                def load_down(e):
                    w = a["L0_ffn_w_down"]
                    sp.dma_start(dnst[:, 0:IT - 1, :], w[bass.ds(e, 1), 0:(IT - 1) * P, :]
                                 .rearrange("o (k p) d -> p (o k) d", p=P)).then_inc(dn_in, 16)
                    sp.dma_start(dnst[0:IR, IT - 1, :], w[bass.ds(e, 1), (IT - 1) * P:, :]
                                 .rearrange("o p d -> p (o d)")).then_inc(dn_in, 16)

                def rows_out(n, c):
                    sp.wait_ge(m_read, n * NTASK + (TURN[c] + 1 + PRE))
                    sp.dma_start(s.maxima[c, :, :, :].rearrange("r q p -> q r p"), mrow[c][:, :, :]).then_inc(max_out, 16)

                def rows_in(n, u, c):
                    sp.wait_ge(max_out, n * 32 + (c + 1) * 16)
                    sp.dma_start(qst[u][ROWS:ROWS + 2, :, c * TB:(c + 1) * TB],
                                 s.maxima[c, :, :, :].rearrange("r (h i) p -> r h (i p)", h=GH)).then_inc(max_in[c], 16)

                def step(n, u, m, left):
                    if left > 0:
                        sp.wait_ge(p_free, n * NS + PRE)
                        load_v(n + 1, 1 - u)
                    rows_out(n, 1)
                    rows_in(n, u, 1)
                    if u == 0:
                        sp.wait_ge(dn_step, m * 6)
                        load_down(m)
                    elif left > 0:
                        sp.wait_ge(gu_step, (m + 1) * 6)
                        load_gate_up(m + 1)
                    sp.dma_start(s.xs.rearrange("j p d -> (j p d)")[bass.ds(n * (XS_EACH * P * D), XS_EACH * P * D)]
                                 .rearrange("(p r c) -> p r c", p=P, c=P),
                                 clear[:, :].rearrange("p (o d) -> p o d", o=1).to_broadcast([P, XS_EACH * KT, P]))\
                      .then_inc(xs_clear, 16)
                    if left > 0:
                        rows_out(n + 1, 0)
                        rows_in(n + 1, 1 - u, 0)
                    if left > 1:
                        sp.wait_ge(s_ps, (n + 1) * (2 * NS))
                        load_qk(n + 2, u)

                load_qk(0, 0)
                load_v(0, 0)
                load_qk(1, 1)
                load_gate_up(0)
                sp.wait_ge(clear_set, 1)
                rows_out(0, 0)
                rows_in(0, 0, 0)
                with sp.Fori(0, N // 2 - 1) as m:
                    step(m * 2, 0, m, 2)
                    step(m * 2 + 1, 1, m, 2)
                step(N - 2, 0, N // 2 - 1, 1)
                step(N - 1, 1, N // 2 - 1, 0)
                sp.wait_ge(xs_clear, N * 16)

            @block.gpsimd
            def _(pool):
                for t, value in ((zero, 0.0), (ones, 1.0), (scale, WS), (one, 1.0), (gate_op, 0.0)):
                    pool.memset(t[:, :], value).then_inc(consts, 1)
                pool.wait_ge(consts, 7)
                for t in (ident, identb):
                    pool.affine_select(out=t[:, :], in_=zero[:, :], compare_op=ALU.not_equal, fill=1.0,
                                       base=0, pattern=[[-1, P]], channel_multiplier=1).then_inc(consts, 1)
                pool.affine_select(out=mask_m[:, :], in_=zero[:, :], compare_op=ALU.is_ge, fill=NEG,
                                   base=0, pattern=[[-1, P]], channel_multiplier=1).then_inc(consts, 1)
                pool.affine_select(out=mask_s[:, :], in_=zero[:, :], compare_op=ALU.is_ge, fill=NEG,
                                   base=0, pattern=[[1, P]], channel_multiplier=-1).then_inc(consts, 1)
                pool.tensor_tensor(gate_op[:, :], one[:, :], one[:, :], ALU.mult).then_inc(o_split, 2 * HALF)

                def split(e, parts, step, base):
                    for x, (src, hi, lo) in enumerate(parts):
                        by = scale[0:src.shape[0], :].to_broadcast(list(src.shape))
                        pool.tensor_tensor(hi, src, by, ALU.mult).then_inc(step, 1)
                    for x, (src, hi, lo) in enumerate(parts):
                        pool.wait_ge(step, base + (x + 1))
                        by = scale[0:src.shape[0], :].to_broadcast(list(src.shape))
                        pool.tensor_tensor(src, src, by, ALU.mult).then_inc(step, 1)
                    for x, (src, hi, lo) in enumerate(parts):
                        pool.wait_ge(step, base + (x + 3))
                        pool.tensor_tensor(lo, src, hi, ALU.subtract).then_inc(step, 1)

                def split_gate_up(e):
                    pool.wait_ge(gu_in, e * 32 + 32)
                    split(e, [(gust[:, w, :, :], rgu[:, bass.ds(e, 1), :, 0, w, :].rearrange("p o k i -> p (o k) i"),
                               rgu[:, bass.ds(e, 1), :, 1, w, :].rearrange("p o k i -> p (o k) i")) for w in range(2)],
                          gu_step, e * 6)

                def split_down(e):
                    pool.wait_ge(dn_in, e * 32 + 32)
                    split(e, [(dnst[:, 0:IT - 1, :], rdn[:, bass.ds(e, 1), 0:IT - 1, 0, :].rearrange("p o k i -> p (o k) i"),
                               rdn[:, bass.ds(e, 1), 0:IT - 1, 1, :].rearrange("p o k i -> p (o k) i")),
                              (dnst[0:IR, IT - 1, :], rdn[0:IR, bass.ds(e, 1), IT - 1, 0, :].rearrange("p o i -> p (o i)"),
                               rdn[0:IR, bass.ds(e, 1), IT - 1, 1, :].rearrange("p o i -> p (o i)"))],
                          dn_step, e * 6)

                def split_output(n, c):
                    base = n * 2 * HALF + (2 * c + 2 * HALF)
                    by = one[:, :].to_broadcast([P, TB])
                    pool.wait_ge(att_out[c], n * 16)
                    pool.wait_ge(rec_ready, (n * HALF + (c + 1)) * PIECES)
                    pool.tensor_tensor(o32[c][:, :], o32[c][:, :], rec[:, :], ALU.mult).then_inc(o_ready, 1)
                    pool.wait_ge(o_ready, n * HALF + (c + 1))
                    pool.tensor_tensor(ohl[c][:, 0, :], o32[c][:, :], by, ALU.mult).then_inc(o_split, 1)
                    pool.wait_ge(o_split, base + 1)
                    pool.tensor_tensor(ohl[c][:, 1, :], o32[c][:, :], ohl[c][:, 0, :], ALU.subtract).then_inc(o_split, 1)
                    pool.wait_ge(o_split, base + 2)
                    pool.tensor_tensor(gate_op[:, :], one[:, :], one[:, :], ALU.mult).then_inc(consts, 1)
                    pool.dma_start(a_v[bass.ds(n, 1), :, :, c * TB:(c + 1) * TB].rearrange("o h p t -> p (o h) t"),
                                   ohl[c][:, :, :]).then_inc(att_out[c], 16)

                with pool.Fori(0, N // 2) as m:
                    split_gate_up(m)
                    split_output(m * 2, 0)
                    split_output(m * 2, 1)
                    split_down(m)
                    split_output(m * 2 + 1, 0)
                    split_output(m * 2 + 1, 1)
                for c in range(HALF):
                    pool.wait_ge(att_out[c], N * 16)

            @block.tensor
            def _(pe):
                def maximum(n, u, t):
                    x = tasks[t]
                    out = pM[t % PRE]
                    if len(x) == 1:
                        c = x[0]
                        if c == 0:
                            pe.wait_ge(m_read, n * NTASK + (t + PRE))
                        else:
                            pe.wait_ge(mx_ready, n + 1)
                            pe.wait_ge(m_read, n * NTASK + (t + 1))
                        pe.transpose(out[0:GH * SUB, 0:P], mx[c][:, :], ident[:, :]).then_inc(m_ps, 1)
                        return
                    c, h, i, k0, w, diagonal = x
                    pe.wait_ge(m_read, n * NTASK + (t + 1))
                    mm = pe.matmul(out[:, 0:w], qst[u][0:ROWS, h, i * P:(i + 1) * P], kst[u][0:ROWS, k0:k0 + w],
                                   start=True, stop=not diagonal)
                    if diagonal:
                        mm = pe.matmul(out[:, w - P:w], identb[:, :], mask_m[:, :], start=False, stop=True)
                    mm.then_inc(m_ps, 1)

                def scores(n, u, k, x):
                    c, j, off, w = cols(k)
                    if x == 0 and j == 0:
                        pe.wait_ge(max_in[c], n * 16 + 16)
                    if not (k == 0 and isinstance(n, int) and n == 0):
                        pe.wait_ge(p_ready, n * (2 * NS) + (2 * k - 1 + x))
                    for y in range(2):
                        mm = pe.matmul(pS[x][:, y, 0:w], kst[u][0:ROWS + 2, j * P:(j + 1) * P],
                                       qst[u][0:ROWS + 2, 2 * x + y, c * TB + off:(c + 1) * TB],
                                       start=True, stop=j < c * SUB)
                        if j >= c * SUB:
                            mm = pe.matmul(pS[x][:, y, 0:P], identb[:, :], mask_s[:, :], start=False, stop=True)
                    mm.then_inc(s_ps, 1)

                def values(n, u, k, what):
                    c, j, off, w = cols(k)
                    first, last = j == 0, j == (c + 1) * SUB - 1
                    if what == 0:
                        pe.wait_ge(p_ready, n * (2 * NS) + (2 * k + 2))
                    if k == 0 and what == 0:
                        pe.wait_ge(v_in[u], steps_done * 32)
                    if first:
                        pe.wait_ge(acc_read, n * (2 * HALF) + (2 * c + what))
                    out, lhs = (pA, vt[u][:, j, :]) if what == 0 else (pD, ones[:, :])
                    for h in range(GH):
                        mm = pe.matmul(out[h * HD:(h + 1) * HD, off:TB], lhs, pb[k % 2][:, h, 0:w],
                                       start=first, stop=last)
                    if what == 1:
                        mm.then_inc(p_free, 1)

                def step(n, u, last):
                    for k in range(NS):
                        if k == START and not last:
                            pe.wait_ge(qk_in[1 - u], (steps_done + u) * (LOADS * 16))
                        for x in range(4):
                            if x < 2 and k + 1 < NS:
                                scores(n, u, k + 1, x)
                            elif x < 2 and not last:
                                scores(n + 1, 1 - u, 0, x)
                            elif x >= 2:
                                values(n, u, k, x - 2)
                            for step_of, t in maxima(n, k, x, last):
                                maximum(step_of, 1 - u if k >= START else u, t)

                pe.wait_ge(consts, NCONST)
                pe.wait_ge(qk_in[0], LOADS * 16)
                for t in range(beside[0][0]):
                    maximum(0, 0, t)
                for x in range(2):
                    scores(0, 0, 0, x)
                with pe.Fori(0, N // 2 - 1) as m:
                    steps_done = m + 1
                    step(m * 2, 0, False)
                    step(m * 2 + 1, 1, False)
                steps_done = N // 2
                step(N - 2, 0, False)
                step(N - 1, 1, True)

            @block.scalar
            def _(act):
                def step(n, first=False):
                    for k in range(NS):
                        c, j, off, w = cols(k)
                        act.wait_ge(p_free, n * NS + (k + 1))
                        for x in range(2):
                            act.wait_ge(s_ps, n * (2 * NS) + (2 * k + x + 1))
                            act.activation(pb[k % 2][:, 2 * x:2 * x + 2, 0:w], pS[x][:, :, 0:w], ACT.Exp,
                                           scale=SCALE).then_inc(p_ready, 1)
                        if k == 0 and not first:
                            leave_psum(n - 1, 1)
                        if k == SUB:
                            leave_psum(n, 0)

                def leave_psum(n, c):
                    k = NS if c == HALF - 1 else SUB
                    act.wait_ge(p_free, n * NS + (k + PRE))
                    act.wait_ge(o_split, n * (2 * HALF) + (2 * c + 2))
                    act.activation(o32[c][:, :], pA[:, :], ACT.Copy).then_inc(acc_read, 1)
                    act.wait_ge(o_ready, n * HALF + c)
                    act.activation(rec[:, :], pD[:, :], ACT.Copy).then_inc(acc_read, 1)

                step(0, True)
                with act.Fori(1, N) as n:
                    step(n)
                leave_psum(N - 1, 1)

            @block.vector
            def _(dve):
                dve.memset(clear[:, :], 0.0).then_inc(clear_set, 1)
                for u in range(2):
                    dve.memset(kst[u][ROWS:ROWS + 2, :], 1.0).then_inc(consts, 1)
                dve.memset(rec[:, 0:1], 0.0).then_inc(m_read, PRE)
                dve.memset(rec[:, 1:2], 0.0).then_inc(p_free, PRE)
                dve.memset(rec[:, 2:3], 0.0).then_inc(acc_read, 1)

                def maximum(n, t):
                    x = tasks[t]
                    src = pM[t % PRE]
                    if len(x) == 1:
                        c = x[0]
                        dve.wait_ge(m_ps, n * NTASK + (t + 1))
                        dve.tensor_scalar(mrow[c][:, 0, :], src[0:GH * SUB, 0:P], -1.0, None, ALU.mult).then_inc(m_neg, 1)
                        dve.wait_ge(m_neg, n * HALF + (c + 1))
                        dve.scalar_tensor_tensor(mrow[c][:, 1, :], src[0:GH * SUB, 0:P], -1.0, mrow[c][:, 0, :],
                                                 ALU.mult, ALU.subtract).then_inc(m_read, 1)
                        return
                    c, h, i, k0, w, diagonal = x
                    at = h * SUB + i % SUB
                    to = mx[0][:, at:at + 1] if c == 0 else mxp[:, k0 // TB, at:at + 1]
                    dve.wait_ge(m_ps, n * NTASK + (t + 1))
                    dve.tensor_reduce(to, src[:, 0:w], AX.X, ALU.max).then_inc(m_read, 1)
                    if t + 1 == TURN[1]:
                        dve.wait_ge(m_read, n * NTASK + (t + 1 + PRE))
                        dve.tensor_tensor(mx[1][:, :], mxp[:, 0, :], mxp[:, 1, :], ALU.max).then_inc(mx_ready, 1)

                def invert(n, c, i):
                    if i == 0:
                        dve.wait_ge(acc_read, n * (2 * HALF) + (2 * c + 3))
                    part = rec[:, i * TB // PIECES:(i + 1) * TB // PIECES]
                    dve.reciprocal(part, part).then_inc(rec_ready, 1)

                def step(n, last, first=False):
                    for k in range(NS):
                        for x in range(4):
                            for step_of, t in maxima(n, k, x, last):
                                maximum(step_of, t)
                            if k in (1, 2) and not first:
                                invert(n - 1, 1, (k - 1) * 4 + x)
                            if k in (SUB + 1, SUB + 2):
                                invert(n, 0, (k - SUB - 1) * 4 + x)

                for t in range(beside[0][0]):
                    maximum(0, t)
                step(0, False, True)
                with dve.Fori(1, N - 1) as n:
                    step(n, False)
                step(N - 1, True)
                for i in range(PIECES):
                    invert(N - 1, 1, i)


class Routing:

    def __init__(self, ctx, nc):
        def sb(name, shape, dt):
            return ctx.enter_context(nc.sbuf_tensor(name, shape, dt))

        self.logits = sb("logits", [P, NT, NR], fp32)
        self.slots = sb("slots", [P, TOPK, NT], u32)
        self.weights = sb("weights", [P, TOPK, NT], fp32)
        self.shared = sb("shared_w", [P, NT], fp32)
        self.expert_at = sb("expert_at", [1, NX], i32)


def project_and_route(nc, a, s, ro):
    V = 4
    PAIRS = NT // 2
    with ExitStack() as ctx:
        def sb(name, shape, dt):
            return ctx.enter_context(nc.sbuf_tensor(name, shape, dt))

        def sem(name):
            return ctx.enter_context(nc.semaphore(name))

        work = sb("work3", [P, 4, D], fp32)
        wst, zt, h2 = work, [work[:, v, :] for v in range(2)], [work[:, 2 + v, :] for v in range(2)]
        wo = sb("wo_split", [P, 2, KT, D], fp16)
        mod = sb("mod_bc", [P, B, 3, D], fp32)
        rw = sb("router_w", [P, KT, NR], fp32)
        ident = sb("ident3", [P, P], fp32)
        eps = sb("eps3", [P, 1], fp32)
        at = [sb(f"at{q}", [P, NKV, 2, 2 * P], fp16) for q in range(2)]
        xt = [sb(f"x3_{v}", [P, D], fp32) for v in range(V)]
        gated = [sb(f"gated{v}", [P, D], fp32) for v in range(2)]
        ht = [sb(f"ht_{v}", [P, KT, P], fp32) for v in range(2)]
        hs = [sb(f"hs_{v}", [P, KT, 2, P], fp16) for v in range(2)]
        st = [sb(f"st3_{v}", [P, 6], fp32) for v in range(2)]
        mv = sb("mv3", [P, 2, 2], fp32)
        tick = sb("tick3", [P, 1], fp32)
        sd = sb("sd3", [P, 2], fp32)
        rs = sb("rs3", [P, 2], fp32)
        lg = ro.logits
        pY = [ctx.enter_context(nc.psum_tensor(f"pY3_{v}", [P, D], fp32)) for v in range(V)]
        pT = [ctx.enter_context(nc.psum_tensor(f"pT3_{v}", [P, KT, P], fp32)) for v in range(2)]
        pL = [ctx.enter_context(nc.psum_tensor(f"pL3_{v}", [P, TB], fp32)) for v in range(2)]

        consts, wo_in, mod0_in, mod_in, rw_in, wo_high, wo_low = (sem(n) for n in (
            "consts3", "wo_in", "mod0_in", "mod_in", "rw_in", "wo_high", "wo_low"))
        at_in = [sem(f"at_in{q}") for q in range(2)]
        x_in = [sem(f"x_in3_{v}") for v in range(V)]
        y_ps, y_gated, x1_ready, stats, aggr, sd_ready, rs_ready, z_ready = (sem(n + "3") for n in (
            "y_ps", "y_gated", "x1_ready", "stats", "aggr", "sd_ready", "rs_ready", "z_ready"))
        h2_step, h_turned, ht_ready, ht_high, ht_low, l_ps, l_read = (sem(n + "3") for n in (
            "h2_step", "h_turned", "ht_ready", "ht_high", "ht_low", "l_ps", "l_read"))
        x1_out = [sem(f"x1_out{v}") for v in range(V)]
        h2_out = [sem(f"h2_out{v}") for v in range(2)]
        hs_out = [sem(f"hs_out{v}") for v in range(2)]

        x_v = a["L0_attn_x"].rearrange("b (n p) d -> (b n) p d", p=P)
        TPB = S // P

        def load_attention(engine, pair, q):
            engine.dma_start(at[q][:, :, :, :].rearrange("p g h t -> p (g h) t"),
                             s.att.rearrange("b g h p t -> b p (g h) t")
                             [bass.ds(pair // (TPB // 2), 1), :, :, bass.ds(pair % (TPB // 2) * (2 * P), 2 * P)]
                             .rearrange("o p g t -> p (o g) t")).then_inc(at_in[q], 16)

        with nc.Block() as block:
            @block.sync
            def _(sp):
                def load_x(n, v):
                    sp.dma_start(xt[v][:, :], x_v[bass.ds(n, 1), :, :].rearrange("o p d -> p (o d)")).then_inc(x_in[v], 16)

                sp.dma_start(wst[:, :, :], a["L0_attn_Wo"].rearrange("(k p) d -> p k d", p=P)).then_inc(wo_in, 16)
                load_attention(sp, 0, 0)
                load_attention(sp, 1, 1)
                for i, j in enumerate((2, 3, 4)):
                    sp.dma_start(mod[:, 0, i, :], s.mod[0, j:j + 1, :].to_broadcast([P, D])).then_inc(mod0_in, 16)
                for v in range(V):
                    load_x(v, v)
                for k in range(KT):
                    sp.dma_start(rw[:, k, 0:E], a["L0_ffn_router_w"][:, k * P:(k + 1) * P].rearrange("e p -> p e"),
                                 allow_slow_non_contiguous=True).then_inc(rw_in, 16)
                    sp.dma_start(rw[:, k, E:NR], a["L0_ffn_shared_gate_w"][k * P:(k + 1) * P].rearrange("(p o) -> p o", o=1))\
                      .then_inc(rw_in, 16)

                for b in range(1, B):
                    for i, j in enumerate((2, 3, 4)):
                        sp.dma_start(mod[:, b, i, :], s.mod[b, j:j + 1, :].to_broadcast([P, D])).then_inc(mod_in, 16)

                def step(i, last):
                    for q in range(V // 2):
                        for w in range(2):
                            v = 2 * q + w
                            sp.wait_ge(x1_ready, i * V + (v + 1))
                            sp.dma_start(s.x1[bass.ds(i * V + v, 1), :, :].rearrange("o p d -> p (o d)"), xt[v][:, :])\
                              .then_inc(x1_out[v], 16)
                        for w in range(2):
                            n = i * V + (2 * q + w)
                            sp.wait_ge(h2_step, n * 2 + 2)
                            sp.dma_start(s.h2[bass.ds(n, 1), :, :].rearrange("o p d -> p (o d)"), h2[w]).then_inc(h2_out[w], 16)
                        for w in range(2):
                            v = 2 * q + w
                            if not last:
                                sp.wait_ge(x1_out[v], i * 16 + 16)
                                load_x((i + 1) * V + v, v)
                        for w in range(2):
                            n = i * V + (2 * q + w)
                            sp.wait_ge(ht_low, n + 1)
                            sp.dma_start(s.h2T[bass.ds(n, 1), :, :, :, :].rearrange("o p k h t -> p (o k h t)"),
                                         hs[w][:, :, :, :].rearrange("p k h t -> p (k h t)")).then_inc(hs_out[w], 16)

                with sp.Fori(0, NT // V - 1) as i:
                    step(i, False)
                step(NT // V - 1, True)
                for v in range(V):
                    sp.wait_ge(x1_out[v], NT // V * 16)
                for w in range(2):
                    sp.wait_ge(h2_out[w], NT // 2 * 16)
                    sp.wait_ge(hs_out[w], NT // 2 * 16)

            @block.gpsimd
            def _(pool):
                pool.memset(ident[:, :], 0.0).then_inc(consts, 1)
                pool.memset(eps[:, :], EPS).then_inc(consts, 1)
                pool.wait_ge(consts, 2)
                pool.affine_select(out=ident[:, :], in_=ident[:, :], compare_op=ALU.not_equal, fill=1.0,
                                   base=0, pattern=[[-1, P]], channel_multiplier=1).then_inc(consts, 1)

                def modulate(i):
                    for w in range(2):
                        n = i * 2 + w
                        b = n // TPB
                        pool.wait_ge(h2_out[w], i * 16)
                        pool.wait_ge(h_turned, i * 2)
                        pool.wait_ge(z_ready, n + 1)
                        pool.tensor_tensor(h2[w], zt[w], mod[:, bass.ds(b, 1), 2, :].rearrange("p o d -> p (o d)"),
                                           ALU.mult).then_inc(h2_step, 1)
                        pool.wait_ge(h2_step, n * 2 + 1)
                        pool.tensor_tensor(h2[w], h2[w], mod[:, bass.ds(b, 1), 1, :].rearrange("p o d -> p (o d)"),
                                           ALU.add).then_inc(h2_step, 1)

                pool.wait_ge(mod0_in, 3 * 16)
                for i in range(2):
                    modulate(i)
                pool.wait_ge(mod_in, 3 * (B - 1) * 16)
                with pool.Fori(2, PAIRS) as i:
                    modulate(i)

            @block.tensor
            def _(pe):
                def project(n, i, v):
                    if v % 2 == 0:
                        pe.wait_ge(at_in[v // 2], i * 16 + 16)
                    if not (isinstance(i, int) and i == 0):
                        pe.wait_ge(y_gated, n - (V - 1))
                    for g in range(KT):
                        for ah, wh in ((0, 0), (0, 1), (1, 0)):
                            mm = pe.matmul(pY[v][:, :], at[v // 2][:, g, ah, v % 2 * P:(v % 2 + 1) * P], wo[:, wh, g, :],
                                           start=g == 0 and (ah, wh) == (0, 0), stop=g == KT - 1 and ah == 1)
                    mm.then_inc(y_ps, 1)

                def turn(n, w):
                    pe.wait_ge(h2_step, n * 2 + 2)
                    pe.wait_ge(ht_high, (n // 2) * 2)
                    for k in range(KT):
                        mm = pe.transpose(pT[w][:, k, :], h2[w][:, k * P:(k + 1) * P], ident[:, :])
                    mm.then_inc(h_turned, 1)

                def route(n, w):
                    pe.wait_ge(ht_ready, n + 1)
                    pe.wait_ge(l_read, (n // 2) * 2)
                    for k in range(KT):
                        mm = pe.matmul(pL[w][:, 0:NR], ht[w][:, k, :], rw[:, k, :], start=k == 0, stop=k == KT - 1)
                    mm.then_inc(l_ps, 1)

                def step(i, last):
                    for p in range(V // 2):
                        for v in (2 * p, 2 * p + 1):
                            turn(i * V + v, v % 2)
                        for v in (2 * p, 2 * p + 1):
                            if not last:
                                project((i + 1) * V + v, i + 1, v)
                        for v in (2 * p, 2 * p + 1):
                            route(i * V + v, v % 2)

                pe.wait_ge(wo_low, 1)
                for v in range(V):
                    project(v, 0, v)
                pe.wait_ge(consts, 3)
                pe.wait_ge(rw_in, 2 * KT * 16)
                with pe.Fori(0, NT // V - 1) as i:
                    step(i, False)
                step(NT // V - 1, True)

            @block.scalar
            def _(act):
                act.wait_ge(wo_in, 16)
                act.activation(wo[:, 0, :, :], wst[:, :, :], ACT.Copy, scale=WS).then_inc(wo_high, 1)
                act.wait_ge(consts, 3)

                def deviation(i):
                    act.wait_ge(aggr, i + 1)
                    act.activation(sd[:, :], mv[:, :, 1], ACT.Sqrt, bias=eps[:, :]).then_inc(sd_ready, 1)

                def pair(i, q, left):
                    for w in range(2):
                        n = i * 2 + w
                        act.wait_ge(h_turned, n + 1)
                        act.wait_ge(ht_low, i * 2)
                        act.wait_ge(l_ps, i * 2)
                        act.activation(ht[w][:, :, :], pT[w][:, :, :], ACT.Copy).then_inc(ht_ready, 1)
                        act.wait_ge(hs_out[w], i * 16)
                        act.activation(hs[w][:, :, 0, :], pT[w][:, :, :], ACT.Copy).then_inc(ht_high, 1)
                    for w in range(2):
                        n = i * 2 + w
                        act.wait_ge(l_ps, n + 1)
                        act.activation(lg[:, bass.ds(n, 1), :].rearrange("p o r -> p (o r)"), pL[w][:, 0:NR], ACT.Copy)\
                           .then_inc(l_read, 1)
                    if left > 3:
                        load_attention(act, i + 4, q)
                    if left > 1:
                        deviation(i + 2)

                deviation(0)
                deviation(1)
                act.wait_ge(y_ps, V)
                for q in range(2):
                    load_attention(act, q + 2, q)
                with act.Fori(0, PAIRS // 2 - 2) as j:
                    for q in range(2):
                        pair(j * 2 + q, q, 4)
                for i in range(PAIRS - 4, PAIRS):
                    pair(i, i % 2, PAIRS - i - 1)

            @block.vector
            def _(dve):
                dve.wait_ge(wo_high, 1)
                dve.scalar_tensor_tensor(wo[:, 1, :, :], wst[:, :, :], WS, wo[:, 0, :, :], ALU.mult, ALU.subtract)\
                   .then_inc(wo_low, 1)
                dve.wait_ge(mod0_in, 3 * 16)
                dve.wait_ge(consts, 2)

                def norm(i, pair, q):
                    tiles = [(pair * 2 + w, 2 * q + w, w) for w in range(2)]
                    for n, v, w in tiles:
                        dve.wait_ge(y_ps, n + 1)
                        dve.scalar_tensor_tensor(gated[w][:, :], pY[v][:, :], 1 / WS,
                                                 mod[:, bass.ds(n // TPB, 1), 0, :].rearrange("p o d -> p (o d)"),
                                                 ALU.mult, ALU.mult).then_inc(y_gated, 1)
                    for n, v, w in tiles:
                        dve.wait_ge(x_in[v], i * 16 + 16)
                        dve.wait_ge(y_gated, n + 1)
                        dve.tensor_tensor(xt[v][:, :], gated[w][:, :], xt[v][:, :], ALU.add).then_inc(x1_ready, 1)
                    for n, v, w in tiles:
                        dve.wait_ge(x1_ready, n + 1)
                        dve.bn_stats(st[w][:, :], xt[v][:, :]).then_inc(stats, 1)
                    dve.wait_ge(stats, pair * 2 + 2)
                    dve.tensor_copy(tick[:, :], eps[:, :])
                    for w in range(2):
                        op = dve.bn_aggr(mv[:, w, :], st[w][:, :])
                    op.then_inc(aggr, 1)
                    dve.wait_ge(sd_ready, pair + 1)
                    dve.reciprocal(rs[:, :], sd[:, :]).then_inc(rs_ready, 1)
                    dve.wait_ge(rs_ready, pair + 1)
                    for n, v, w in tiles:
                        dve.wait_ge(h2_step, pair * 4)
                        dve.tensor_scalar(zt[w], xt[v][:, :], mv[:, w, 0:1], rs[:, w:w + 1],
                                          ALU.subtract, ALU.mult).then_inc(z_ready, 1)

                def low(pair):
                    for w in range(2):
                        dve.wait_ge(ht_high, pair * 2 + (w + 1))
                        dve.tensor_tensor(hs[w][:, :, 1, :], ht[w][:, :, :], hs[w][:, :, 0, :], ALU.subtract).then_inc(ht_low, 1)

                for q in range(2):
                    norm(0, q, q)
                dve.wait_ge(mod_in, 3 * (B - 1) * 16)
                with dve.Fori(0, PAIRS // 2 - 1) as i:
                    for q in range(2):
                        low(i * 2 + q)
                        norm(i + 1, i * 2 + (q + 2), q)
                for q in range(2):
                    low(PAIRS - 2 + q)


def choose_and_scatter(nc, s, ro):
    RING = 4
    SL = FIRST * ST
    COUNT = 4
    with ExitStack() as ctx:
        def sb(name, shape, dt):
            return ctx.enter_context(nc.sbuf_tensor(name, shape, dt))

        def sem(name):
            return ctx.enter_context(nc.semaphore(name))

        lg = ro.logits
        top = sb("top", [P, NT, 8], fp32)
        top_at = sb("top_at", [P, NT, 8], u32)
        choice = sb("choice", [P, TOPK, NT], fp32)
        iota_e = sb("iota_e", [P, E], fp32)
        iota_j = sb("iota_j", [P, NX], fp32)
        one_hot = [sb(f"one_hot{c}", [P, NT, E], fp32) for c in range(TOPK)]
        chosen = sb("chosen", [P, NT, E], bf16)
        before = sb("before", [P, P], bf16)
        ones = sb("ones4", [P, P], bf16)
        scan = [sb(f"scan{x}", [P, NT, E], fp32) for x in range(2)]
        total = sb("total", [P, NT, E], fp32)
        place = sb("place", [P, NT, E], fp32)
        part = sb("part", [P, NT, E], fp32)
        slot = sb("slot", [P, TOPK, NT], fp32)
        count = sb("count", [P, E], fp32)
        count_i = sb("count_i", [P, E], i32)
        tiles = sb("tiles", [P, E], fp32)
        end = [sb(f"end{x}", [P, E], fp32) for x in range(2)]
        after = sb("after", [P, NX, E], fp32)
        tile_e = sb("tile_e", [P, NX], fp32)
        diff = sb("diff", [P, NT], fp32)
        low = sb("low_w", [P, NT], fp32)
        gate = sb("gate_w", [P, NT], fp32)
        hr = [sb(f"hr{v}", [P, D], fp32) for v in range(RING)]
        wgu = [sb(f"wgu4_{x}", [P, KT, 2, 2, P], fp16) for x in range(2)]
        wdn = [sb(f"wdn4_{x}", [P, 2, D], fp16) for x in range(2)]
        hT = [sb(f"hT4_{n}", [P, SUB, KT, 2, P], fp16) for n in range(FIRST)]
        th = sb("th4", [P, TB], fp32)
        hb = sb("hb4", [P, TB], fp32)
        sT = [sb(f"sT4_{x}", [P, 2, TB], fp16) for x in range(2)]
        yb = [sb(f"yb4_{t}", [P, D], fp32) for t in range(SUB)]
        pG = [[ctx.enter_context(nc.psum_tensor(f"pG4_{x}{w}", [P, TB], fp32)) for w in range(2)] for x in range(2)]
        pY = [ctx.enter_context(nc.psum_tensor(f"pY4_{t}", [P, D], fp32)) for t in range(SUB)]

        ready, consts, exps, step = sem("chosen_ready"), sem("consts4"), sem("exps4"), sem("step4")
        counted, count_read, slots_ready = sem("counted"), sem("count_read"), sem("slots_ready")
        hr_in = [sem(f"hr_in{v}") for v in range(RING)]
        hr_out = [sem(f"hr_out{v}") for v in range(RING)]
        gu_in, dn_in = ([sem(f"{n}_in4_{x}") for x in range(2)] for n in ("gu", "dn"))
        h_in = [sem(f"h_in4_{n}") for n in range(FIRST)]
        gu_ps, th_ready, gt_ready, hb_ready, s_high, s_low, y_ps, y_read = (sem(n + "4") for n in (
            "gu_ps", "th_ready", "gt_ready", "hb_ready", "s_high", "s_low", "y_ps", "y_read"))
        y_out = [sem(f"y_out4_{t}") for t in range(SUB)]
        counts = pG[(COUNT + 1) % 2][0][:, :].rearrange("p (x t e) -> p x t e", x=2, e=E)
        xs_flat = s.xs.rearrange("j p d -> (j p) d")

        with nc.Block() as block:
            @block.sync
            def _(sp):
                def load_h(n):
                    sp.dma_start(hT[n][:, :, :, :, :].rearrange("p s k h t -> p s (k h t)"),
                                 s.h2T[n * SUB:(n + 1) * SUB, :, :, :, :].rearrange("s p k h t -> p s (k h t)")).then_inc(h_in[n], 16)

                def load_gate_up(m):
                    sp.dma_start(wgu[m % 2][:, :, :, :, :], s.sgu[m % ST, :, :, :, :, :]).then_inc(gu_in[m % 2], 16)

                def load_down(m):
                    sp.dma_start(wdn[m % 2][:, :, :], s.sdn[m % ST, :, :, :]).then_inc(dn_in[m % 2], 16)

                def load_rows(n):
                    v = n % RING
                    if n >= RING:
                        sp.wait_ge(hr_out[v], n // RING * (TOPK * 16))
                    sp.dma_start(hr[v][:, :], s.h2[n, :, :]).then_inc(hr_in[v], 16)

                load_h(0)
                for m in range(2):
                    load_gate_up(m)
                    load_down(m)
                load_h(1)
                for n in range(RING):
                    load_rows(n)
                rows = RING
                for m in range(SL):
                    if m + 2 < SL:
                        sp.wait_ge(gu_ps, m + 1)
                        load_gate_up(m + 2)
                        sp.wait_ge(y_ps, m + 1)
                        load_down(m + 2)
                    for _ in range(3 if m >= COUNT + 2 else 0):
                        if rows < NT:
                            load_rows(rows)
                            rows += 1
                assert rows == NT

            @block.gpsimd
            def _(pool):
                pool.iota(iota_e[:, :], pattern=[[1, E]], base=0, channel_multiplier=0,
                          allow_small_or_imprecise_dtypes=True).then_inc(consts, 1)
                pool.iota(iota_j[:, :], pattern=[[1, NX]], base=0, channel_multiplier=0,
                          allow_small_or_imprecise_dtypes=True).then_inc(consts, 1)
                pool.memset(ones[:, :], 1.0).then_inc(consts, 1)
                pool.wait_ge(consts, 3)
                pool.affine_select(out=before[:, :], in_=ones[:, :], compare_op=ALU.is_gt, fill=0.0,
                                   base=0, pattern=[[1, P]], channel_multiplier=-1).then_inc(consts, 1)
                pool.wait_ge(slots_ready, 1)
                for n in range(NT):
                    v = n % RING
                    pool.wait_ge(hr_in[v], (n // RING + 1) * 16)
                    for c in range(TOPK):
                        pool.indirect_dma_start(out=xs_flat, out_offset=bass.IndirectOffsetOnAxis(ap=ro.slots[:, c, n:n + 1], axis=0),
                                                in_=hr[v][:, :], in_offset=None).then_inc(hr_out[v], 16)
                for v in range(RING):
                    pool.wait_ge(hr_out[v], NT // RING * TOPK * 16)

            @block.tensor
            def _(pe):
                def gate_up(m):
                    n, x = m // ST, m % 2
                    if m % ST == 0:
                        pe.wait_ge(h_in[n], 16)
                    pe.wait_ge(gu_in[x], (m // 2 + 1) * 16)
                    if m >= 2:
                        pe.wait_ge(hb_ready, m - 1)
                    for k in range(KT):
                        for w in range(2):
                            for wh, hh in ((0, 0), (0, 1), (1, 0)):
                                mm = pe.matmul(pG[x][w][:, :], wgu[x][:, k, w, wh, :], hT[n][:, :, k, hh, :],
                                               start=k == 0 and (wh, hh) == (0, 0), stop=k == KT - 1 and wh == 1)
                    mm.then_inc(gu_ps, 1)

                def down(m):
                    i, x = m % ST, m % 2
                    pe.wait_ge(dn_in[x], (m // 2 + 1) * 16)
                    pe.wait_ge(s_low, m + 1)
                    if i == 0 and m:
                        pe.wait_ge(y_read, m // ST * SUB)
                    for t in range(SUB):
                        for sh, wh in ((0, 0), (0, 1), (1, 0)):
                            mm = pe.matmul(pY[t][:, :], sT[x][:, sh, t * P:(t + 1) * P], wdn[x][:, wh, :],
                                           start=i == 0 and (sh, wh) == (0, 0), stop=i == ST - 1 and sh == 1)
                    mm.then_inc(y_ps, 1)

                gate_up(0)
                for m in range(SL):
                    if m != COUNT:
                        if m + 1 < SL:
                            gate_up(m + 1)
                        down(m)
                    else:
                        pe.wait_ge(consts, 4)
                        pe.wait_ge(ready, 1)
                        pe.wait_ge(hb_ready, m)
                        flat = chosen[:, :, :].rearrange("p t e -> p (t e)")
                        for y, lhs in enumerate((before, ones)):
                            pe.matmul(counts[:, y, :, :].rearrange("p t e -> p (t e)"), lhs[:, :], flat,
                                      start=True, stop=True).then_inc(counted, 1)
                        down(m)
                        pe.wait_ge(count_read, 1)
                        gate_up(m + 1)

            @block.scalar
            def _(act):
                def part(m):
                    act.wait_ge(gu_ps, m + 1)
                    act.activation(th[:, :], pG[m % 2][0][:, :], ACT.Tanh, scale=0.5 / WS).then_inc(th_ready, 1)
                    act.wait_ge(hb_ready, m + 1)
                    if m >= 2:
                        act.wait_ge(y_ps, m - 1)
                    act.activation(sT[m % 2][:, 0, :], hb[:, :], ACT.Copy).then_inc(s_high, 1)

                def results(n):
                    act.wait_ge(y_ps, (n + 1) * ST)
                    for t in range(SUB):
                        k = n * SUB + t
                        if n:
                            act.wait_ge(y_out[t], n * 16)
                        act.activation(yb[t][:, :], pY[t][:, :], ACT.Copy).then_inc(y_read, 1)
                        act.wait_ge(y_read, k + 1)
                        act.dma_start(s.shy[k, :, :], yb[t][:, :]).then_inc(y_out[t], 16)

                part(0)
                for m in range(SL):
                    if m + 1 < SL:
                        part(m + 1)
                    if m == 1:
                        act.wait_ge(exps, 1)
                        act.activation(low[:, :], diff[:, :], ACT.Exp).then_inc(exps, 1)
                        act.activation(gate[:, :], lg[:, :, E], ACT.Exp, scale=-1.0).then_inc(exps, 1)
                    if m % ST == ST - 1:
                        results(m // ST)
                for t in range(SUB):
                    act.wait_ge(y_out[t], FIRST * 16)

            @block.vector
            def _(dve):
                done = [0]

                def link(op):
                    done[0] += 1
                    op.then_inc(step, 1)
                    dve.wait_ge(step, done[0])

                def share(m):
                    x = m % 2
                    dve.wait_ge(th_ready, m + 1)
                    dve.scalar_tensor_tensor(th[:, :], th[:, :], 1.0, pG[x][0][:, :], ALU.add, ALU.mult).then_inc(gt_ready, 1)
                    dve.wait_ge(gt_ready, m + 1)
                    dve.scalar_tensor_tensor(hb[:, :], th[:, :], 0.5 / (WS * WS), pG[x][1][:, :], ALU.mult, ALU.mult)\
                       .then_inc(hb_ready, 1)
                    dve.wait_ge(s_high, m + 1)
                    dve.tensor_tensor(sT[x][:, 1, :], hb[:, :], sT[x][:, 0, :], ALU.subtract).then_inc(s_low, 1)

                share(0)
                for t in range(NT):
                    op = dve.max(top[:, t, :], lg[:, t, 0:E])
                link(op)
                for t in range(NT):
                    op = dve.max_index(top_at[:, t, :], top[:, t, :], lg[:, t, 0:E])
                link(op)
                share(1)
                dve.tensor_tensor(diff[:, :], top[:, :, 1], top[:, :, 0], ALU.subtract).then_inc(exps, 1)
                link(dve.tensor_copy(choice[:, :, :], top_at[:, :, 0:TOPK].rearrange("p t c -> p c t")))
                dve.wait_ge(consts, 4)
                for c in range(TOPK):
                    op = dve.tensor_tensor(one_hot[c][:, :, :], choice[:, c, :].rearrange("p (t o) -> p t o", o=1).to_broadcast([P, NT, E]),
                                           iota_e[:, :].rearrange("p (o e) -> p o e", o=1).to_broadcast([P, NT, E]), ALU.is_equal)
                link(op)
                dve.tensor_tensor(chosen[:, :, :], one_hot[0][:, :, :], one_hot[1][:, :, :], ALU.add).then_inc(ready, 1)
                share(2)
                dve.wait_ge(exps, 3)
                link(dve.tensor_scalar(diff[:, :], low[:, :], 1.0, None, ALU.add))
                link(dve.reciprocal(ro.weights[:, 0, :], diff[:, :]))
                dve.tensor_tensor(ro.weights[:, 1, :], ro.weights[:, 0, :], low[:, :], ALU.mult)
                link(dve.tensor_scalar(gate[:, :], gate[:, :], 1.0, None, ALU.add))
                link(dve.reciprocal(diff[:, :], gate[:, :]))
                dve.tensor_scalar(ro.shared[:, :], diff[:, :], 1 / WS, None, ALU.mult)
                share(3)
                share(COUNT)
                dve.wait_ge(counted, 2)
                dve.tensor_copy(place[:, :, :], counts[:, 0, :, :])
                dve.tensor_copy(scan[0][:, :, :], counts[:, 1, :, :]).then_inc(count_read, 1)
                dve.wait_ge(count_read, 1)
                link(dve.tensor_copy(total[:, :, :], scan[0][:, :, :]))
                x, d = 0, 1
                while d < NT:
                    dve.tensor_copy(scan[1 - x][:, 0:d, :], scan[x][:, 0:d, :])
                    link(dve.tensor_tensor(scan[1 - x][:, d:, :], scan[x][:, d:, :], scan[x][:, 0:NT - d, :], ALU.add))
                    x, d = 1 - x, 2 * d
                share(COUNT + 1)
                link(dve.tensor_scalar(count[:, :], scan[x][:, NT - 1, :], float(P - 1), None, ALU.add))
                link(dve.tensor_copy(count_i[:, :], count[:, :]))
                link(dve.tensor_single_scalar(count_i[:, :], count_i[:, :], P.bit_length() - 1, ALU.arith_shift_right))
                link(dve.tensor_copy(tiles[:, :], count_i[:, :]))
                link(dve.tensor_copy(end[0][:, :], tiles[:, :]))
                y, d = 0, 1
                while d < E:
                    dve.tensor_copy(end[1 - y][:, 0:d], end[y][:, 0:d])
                    link(dve.tensor_tensor(end[1 - y][:, d:], end[y][:, d:], end[y][:, 0:E - d], ALU.add))
                    y, d = 1 - y, 2 * d
                link(dve.tensor_tensor(tiles[:, :], end[y][:, :], tiles[:, :], ALU.subtract))
                link(dve.tensor_scalar(tiles[:, :], tiles[:, :], float(P), None, ALU.mult))
                link(dve.tensor_tensor(place[:, :, :], place[:, :, :], scan[x][:, :, :], ALU.add))
                link(dve.tensor_tensor(place[:, :, :], place[:, :, :], total[:, :, :], ALU.subtract))
                link(dve.tensor_tensor(place[:, :, :], place[:, :, :],
                                       tiles[:, :].rearrange("p (o e) -> p o e", o=1).to_broadcast([P, NT, E]), ALU.add))
                for c in range(TOPK):
                    link(dve.tensor_tensor(part[:, :, :], place[:, :, :], one_hot[c][:, :, :], ALU.mult))
                    link(dve.tensor_reduce(slot[:, c, :], part[:, :, :], AX.X, ALU.add))
                dve.tensor_copy(ro.slots[:, :, :], slot[:, :, :]).then_inc(slots_ready, 1)
                share(COUNT + 2)
                link(dve.tensor_tensor(after[:, :, :], end[y][:, :].rearrange("p (o e) -> p o e", o=1).to_broadcast([P, NX, E]),
                                       iota_j[:, :].rearrange("p (j o) -> p j o", o=1).to_broadcast([P, NX, E]), ALU.is_le))
                link(dve.tensor_reduce(tile_e[:, :], after[:, :, :], AX.X, ALU.add))
                link(dve.tensor_scalar(tile_e[:, :], tile_e[:, :], float(E - 1), None, ALU.min))
                link(dve.tensor_copy(ro.expert_at[:, :], tile_e[0:1, :]))
                for m in range(COUNT + 3, SL):
                    share(m)


def routed_experts(nc, s, ro, rw):
    STEP = 4
    assert (NX - 3) % STEP == 0
    with ExitStack() as ctx:
        def sb(name, shape, dt):
            return ctx.enter_context(nc.sbuf_tensor(name, shape, dt))

        def sem(name):
            return ctx.enter_context(nc.semaphore(name))

        ident = sb("ident5", [P, P], fp32)
        zero = sb("zero5", [P, P], fp32)
        xs = [sb(f"xs{u}", [P, D], fp32) for u in range(2)]
        xT = sb("xT5", [P, KT, 2, P], fp16)
        th = sb("th5", [P, I], fp32)
        gt = sb("gt5", [P, I], fp32)
        hb = sb("hb5", [P, IT * P], fp32)
        hT = sb("hT5", [P, IT, 2, P], fp16)
        ysb = [sb(f"ysb{u}", [P, D], fp32) for u in range(2)]
        pG = [ctx.enter_context(nc.psum_tensor(f"pG5_{w}", [P, I], fp32)) for w in range(2)]
        pX = ctx.enter_context(nc.psum_tensor("pX5", [P, KT, P], fp32))
        pH = ctx.enter_context(nc.psum_tensor("pH5", [P, IT, P], fp32))
        pY = [ctx.enter_context(nc.psum_tensor(f"pY5_{u}", [P, D], fp32)) for u in range(2)]

        consts = sem("consts5")
        xs_in = [sem("xs_in0"), sem("xs_in1")]
        x_turned, x_high, x_low = sem("x_turned"), sem("x_high5"), sem("x_low5")
        gu_ps, th_ready, gt_ready, hb_ready = sem("gu_ps"), sem("th_ready"), sem("gt_ready"), sem("hb_ready")
        h_turned, h_high, h_low = sem("h_turned5"), sem("h_high5"), sem("h_low5")
        y_ps, y_read, y_out = sem("y_ps5"), sem("y_read5"), [sem("y_out0"), sem("y_out1")]
        rgu, rdn = routed_layout(rw)
        ys_v = s.ys.rearrange("(j p) d -> j p d", p=P)

        with nc.Block() as block:
            @block.sync
            def _(sp):
                def load(j, u):
                    sp.dma_start(xs[u][:, :], s.xs[bass.ds(j, 1), :, :].rearrange("o p d -> p (o d)")).then_inc(xs_in[u], 16)

                def store(j, u):
                    sp.wait_ge(y_read, j + 3)
                    sp.dma_start(ys_v[bass.ds(j, 1), :, :].rearrange("o p d -> p (o d)"), ysb[u][:, :]).then_inc(y_out[u], 16)

                for u in range(2):
                    load(u, u)
                sp.wait_ge(x_turned, 1)
                load(2, 0)
                with sp.Fori(0, (NX - 3) // 2) as i:
                    for u in range(2):
                        sp.wait_ge(x_turned, i * 2 + (u + 2))
                        load(i * 2 + (u + 3), 1 - u)
                        store(i * 2 + u, u)
                for j in range(NX - 3, NX):
                    store(j, j % 2)
                for u in range(2):
                    sp.wait_ge(y_out[u], (NX + 1 - u) // 2 * 16)

            @block.gpsimd
            def _(pool):
                pool.memset(zero[:, :], 0.0).then_inc(consts, 1)
                pool.wait_ge(consts, 1)
                pool.affine_select(out=ident[:, :], in_=zero[:, :], compare_op=ALU.not_equal, fill=1.0,
                                   base=0, pattern=[[-1, P]], channel_multiplier=1).then_inc(consts, 1)

            @block.tensor
            def _(pe):
                def turn_x(j, u):
                    pe.wait_ge(xs_in[u], (j - u) * 8 + 16)
                    pe.wait_ge(x_low, j)
                    for k in range(KT):
                        mm = pe.transpose(pX[:, k, :], xs[u][:, k * P:(k + 1) * P], ident[:, :])
                    mm.then_inc(x_turned, 1)

                def gate_up(j, e):
                    pe.wait_ge(x_low, j + 1)
                    pe.wait_ge(hb_ready, j)
                    for k in range(KT):
                        for xh, wh in ((0, 0), (0, 1), (1, 0)):
                            for w in range(2):
                                mm = pe.matmul(pG[w][:, :], xT[:, k, xh, :],
                                               rgu[:, bass.ds(e, 1), k, wh, w, :].rearrange("p o i -> p (o i)"),
                                               start=k == 0 and (xh, wh) == (0, 0), stop=k == KT - 1 and xh == 1)
                    mm.then_inc(gu_ps, 1)

                def turn_h(j):
                    pe.wait_ge(hb_ready, j + 1)
                    pe.wait_ge(h_low, j)
                    for k in range(IT):
                        mm = pe.transpose(pH[:, k, :], hb[:, k * P:(k + 1) * P], ident[:, :])
                    mm.then_inc(h_turned, 1)

                def down(j, u, e):
                    pe.wait_ge(h_low, j + 1)
                    pe.wait_ge(y_read, j + 1)
                    for k in range(IT):
                        rows = P if k < IT - 1 else IR
                        for hh, wh in ((0, 0), (0, 1), (1, 0)):
                            mm = pe.matmul(pY[u][:, :], hT[0:rows, k, hh, :],
                                           rdn[0:rows, bass.ds(e, 1), k, wh, :].rearrange("p o d -> p (o d)"),
                                           start=k == 0 and (hh, wh) == (0, 0), stop=k == IT - 1 and hh == 1)
                    mm.then_inc(y_ps, 1)

                def experts(j, n):
                    return nc.values_load_multi_w_load_instructions(
                        ro.expert_at[0:1, bass.ds(j, n)], engines=[mybir.EngineType.PE], min_val=0, max_val=E - 1)[1]

                def tile(j, u, last, e_last, e):
                    gate_up(j, e)
                    if not last:
                        turn_x(j + 1, 1 - u)
                    down(j - 1, 1 - u, e_last)
                    turn_h(j)

                pe.wait_ge(consts, 2)
                turn_x(0, 0)
                gate_up(0, experts(0, 1)[0])
                turn_x(1, 1)
                turn_h(0)
                with pe.Fori(0, (NX - 3) // STEP) as i:
                    e = experts(i * STEP, STEP + 1)
                    for t in range(STEP):
                        tile(i * STEP + (t + 1), (t + 1) % 2, False, e[t], e[t + 1])
                e = experts(NX - 3, 3)
                tile(NX - 2, 1, False, e[0], e[1])
                tile(NX - 1, 0, True, e[1], e[2])
                down(NX - 1, 0, e[2])

            @block.scalar
            def _(act):
                def sigmoid_part(j):
                    act.wait_ge(gu_ps, j + 1)
                    act.activation(th[:, :], pG[0][:, :], ACT.Tanh, scale=0.5 / WS).then_inc(th_ready, 1)

                def high_x(j):
                    act.wait_ge(x_turned, j + 1)
                    act.activation(xT[:, :, 0, :], pX[:, :, :], ACT.Copy).then_inc(x_high, 1)

                def high_h(j):
                    act.wait_ge(h_turned, j + 1)
                    act.activation(hT[:, :, 0, :], pH[:, :, :], ACT.Copy).then_inc(h_high, 1)

                def result(j, u, stored):
                    act.wait_ge(y_out[u], stored * 16)
                    act.wait_ge(y_ps, j + 1)
                    act.activation(ysb[u][:, :], pY[u][:, :], ACT.Copy, scale=1 / WS).then_inc(y_read, 1)

                def tile(j, u, stored, last):
                    sigmoid_part(j)
                    if not last:
                        high_x(j + 1)
                    result(j - 1, 1 - u, stored)
                    high_h(j)

                high_x(0)
                sigmoid_part(0)
                high_x(1)
                high_h(0)
                with act.Fori(0, (NX - 3) // 2) as i:
                    tile(i * 2 + 1, 1, i, False)
                    tile(i * 2 + 2, 0, i, False)
                tile(NX - 2, 1, (NX - 3) // 2, False)
                tile(NX - 1, 0, (NX - 3) // 2, True)
                result(NX - 1, 0, (NX - 1) // 2)

            @block.vector
            def _(dve):
                dve.memset(hb[:, I:], 0.0)
                dve.memset(th[:, 0:1], 0.0).then_inc(y_read, 2)

                def mix(j):
                    dve.wait_ge(th_ready, j + 1)
                    dve.scalar_tensor_tensor(gt[:, :], th[:, :], 1.0, pG[0][:, :], ALU.add, ALU.mult).then_inc(gt_ready, 1)
                    dve.wait_ge(gt_ready, j + 1)
                    dve.scalar_tensor_tensor(hb[:, 0:I], gt[:, :], 0.5 / (WS * WS), pG[1][:, :], ALU.mult, ALU.mult)\
                       .then_inc(hb_ready, 1)

                def low_x(j):
                    dve.wait_ge(x_high, j + 1)
                    dve.tensor_tensor(xT[:, :, 1, :], pX[:, :, :], xT[:, :, 0, :], ALU.subtract).then_inc(x_low, 1)

                def low_h(j):
                    dve.wait_ge(h_high, j + 1)
                    dve.tensor_tensor(hT[:, :, 1, :], pH[:, :, :], hT[:, :, 0, :], ALU.subtract).then_inc(h_low, 1)

                def tile(j, last):
                    mix(j)
                    if not last:
                        low_x(j + 1)
                    low_h(j)

                low_x(0)
                mix(0)
                low_x(1)
                low_h(0)
                with dve.Fori(1, NX - 1) as j:
                    tile(j, False)
                tile(NX - 1, True)


def shared_expert_and_sum(nc, a, s, ro, out):
    with ExitStack() as ctx:
        def sb(name, shape, dt):
            return ctx.enter_context(nc.sbuf_tensor(name, shape, dt))

        def sem(name):
            return ctx.enter_context(nc.semaphore(name))

        wgu = sb("wgu6", [P, ST, KT, 2, 2, P], fp16)
        wdn = sb("wdn6", [P, ST, 2, D], fp16)
        gb = sb("gb6", [P, B, D], fp32)
        hT = [sb(f"hT6_{u}", [P, SUB, KT, 2, P], fp16) for u in range(2)]
        th = [sb(f"th6_{u}", [P, TB], fp32) for u in range(2)]
        gt = [sb(f"gt6_{u}", [P, TB], fp32) for u in range(2)]
        hb = [sb(f"hb6_{u}", [P, TB], fp32) for u in range(2)]
        sT = sb("sT6", [P, ST, 2, TB], fp16)
        yg = sb("yg6", [P, SUB, TOPK, D], fp32)
        x1 = sb("x16", [P, SUB, D], fp32)
        rt = [sb(f"rt6_{u}", [P, SUB, D], fp32) for u in range(2)]
        sg = sb("sg6", [P, SUB, D], fp32)
        ye = sb("ye6", [P, TOPK + 1, D], fp32)
        xe = sb("xe6", [P, D], fp32)
        pG = [[ctx.enter_context(nc.psum_tensor(f"pG6_{x}{w}", [P, TB], fp32)) for w in range(2)] for x in range(2)]
        pY = [ctx.enter_context(nc.psum_tensor(f"pY6_{i}", [P, D], fp32)) for i in range(SUB)]

        w_in = [sem(f"w_in6_{i}") for i in range(ST)]
        gb_in, x1_in = sem("gb_in6"), sem("x1_in6")
        ye_in, xe_in, e_step, e_out = sem("ye_in6"), sem("xe_in6"), sem("e_step6"), sem("e_out6")
        h_in = [sem("h_in6_0"), sem("h_in6_1")]
        gu_ps, th_ready, gt_ready, hb_ready, s_high, s_low = (sem(n + "6") for n in (
            "gu_ps", "th_ready", "gt_ready", "hb_ready", "s_high", "s_low"))
        y_ps, y_read, y_in, first_mix, mixed, fin = (sem(n + "6") for n in (
            "y_ps", "y_read", "y_in", "first_mix", "mixed", "fin"))
        stored = [sem("stored6_0"), sem("stored6_1")]
        out_v = out.rearrange("b (n s p) d -> (b n) p s d", s=SUB, p=P)
        MIX = ST // 2
        LATE = NTB - FIRST
        ALONE = FIRST * SUB // (LATE - 2)

        with nc.Block() as block:
            @block.sync
            def _(sp):
                def load_h(n, u):
                    sp.dma_start(hT[u][:, :, :, :, :].rearrange("p s k h t -> p s (k h t)"),
                                 s.h2T[bass.ds(n * SUB + FIRST * SUB, SUB), :, :, :, :].rearrange("s p k h t -> p s (k h t)")).then_inc(h_in[u], 16)

                load_h(0, 0)
                for i in range(ST):
                    sp.dma_start(wgu[:, i, :, :, :, :], s.sgu[i, :, :, :, :, :]).then_inc(w_in[i], 16)
                    sp.dma_start(wdn[:, i, :, :], s.sdn[i, :, :, :]).then_inc(w_in[i], 16)
                load_h(1, 1)
                for b in range(B):
                    sp.dma_start(gb[:, b, :], s.mod[b, 5:6, :].to_broadcast([P, D])).then_inc(gb_in, 16)

                def tile(n, u, last):
                    if not last:
                        sp.wait_ge(gu_ps, (n + 1) * ST)
                        load_h(n + 2, u)
                    sp.wait_ge(fin, n * SUB * 2)
                    sp.dma_start(x1[:, :, :], s.x1[bass.ds(n * SUB + FIRST * SUB, SUB), :, :].rearrange("s p d -> p s d")).then_inc(x1_in, 16)
                    sp.wait_ge(mixed, (n + 1) * SUB)
                    sp.dma_start(out_v[bass.ds(n + FIRST, 1), :, :, :].rearrange("o p s d -> p (o s) d"), rt[u][:, :, :])\
                      .then_inc(stored[u], 16)

                with sp.Fori(0, LATE // 2 - 1) as i:
                    for u in range(2):
                        tile(i * 2 + u, u, False)
                for u in range(2):
                    tile(LATE - 2 + u, u, True)
                for u in range(2):
                    sp.wait_ge(stored[u], LATE // 2 * 16)

            @block.gpsimd
            def _(pool):
                pool.wait_ge(gb_in, B * 16)
                def early(t):
                    for c in range(TOPK):
                        pool.indirect_dma_start(out=ye[:, c, :], out_offset=None, in_=s.ys[:, :],
                                                in_offset=bass.IndirectOffsetOnAxis(ap=ro.slots[:, c, t:t + 1], axis=0)).then_inc(ye_in, 16)
                    pool.dma_start(ye[:, TOPK, :], s.shy[t, :, :]).then_inc(ye_in, 16)
                    pool.wait_ge(e_out, t * 16)
                    pool.dma_start(xe[:, :], s.x1[t, :, :]).then_inc(xe_in, 16)
                    pool.wait_ge(ye_in, (t + 1) * (TOPK + 1) * 16)
                    for c in range(TOPK + 1):
                        by = (ro.weights[:, c, t:t + 1] if c < TOPK else ro.shared[:, t:t + 1]).to_broadcast([P, D])
                        pool.tensor_tensor(ye[:, c, :], ye[:, c, :], by, ALU.mult).then_inc(e_step, 1)
                    done = t * (TOPK + 5) + TOPK + 1
                    pool.wait_ge(e_step, done)
                    for c in range(1, TOPK + 1):
                        pool.tensor_tensor(ye[:, 0, :], ye[:, 0, :], ye[:, c, :], ALU.add).then_inc(e_step, 1)
                        done += 1
                        pool.wait_ge(e_step, done)
                    pool.tensor_tensor(ye[:, 0, :], ye[:, 0, :], gb[:, t * P // S, :], ALU.mult).then_inc(e_step, 1)
                    pool.wait_ge(e_step, done + 1)
                    pool.wait_ge(xe_in, (t + 1) * 16)
                    pool.tensor_tensor(xe[:, :], ye[:, 0, :], xe[:, :], ALU.add).then_inc(e_step, 1)
                    pool.wait_ge(e_step, done + 2)
                    pool.dma_start(out_v[t // SUB, :, t % SUB, :], xe[:, :]).then_inc(e_out, 16)

                for n in range(LATE):
                    u = n % 2
                    pool.wait_ge(first_mix, n * SUB * 2)
                    for i in range(SUB):
                        for c in range(TOPK):
                            at = (FIRST + n) * SUB + i
                            pool.indirect_dma_start(
                                out=yg[:, i, c, :], out_offset=None, in_=s.ys[:, :],
                                in_offset=bass.IndirectOffsetOnAxis(ap=ro.slots[:, c, at:at + 1], axis=0)).then_inc(y_in, 16)
                    if n < LATE - 2:
                        for t in range(n * ALONE, (n + 1) * ALONE):
                            early(t)
                    pool.wait_ge(x1_in, (n + 1) * 16)
                    pool.wait_ge(first_mix, (n + 1) * SUB * 2)
                    for i in range(SUB):
                        pool.tensor_tensor(rt[u][:, i, :], rt[u][:, i, :], gb[:, (n + FIRST) * TB // S, :], ALU.mult).then_inc(fin, 1)
                        pool.wait_ge(fin, (n * SUB + i) * 2 + 1)
                        pool.tensor_tensor(rt[u][:, i, :], rt[u][:, i, :], x1[:, i, :], ALU.add).then_inc(fin, 1)
                pool.wait_ge(e_out, FIRST * SUB * 16)

            @block.tensor
            def _(pe):
                def gate_up(n, u, i, first=False, start=False):
                    x = (u * ST + i) % 2
                    if i == 0:
                        pe.wait_ge(h_in[u], (n - u) * 8 + 16)
                    if first:
                        pe.wait_ge(w_in[i], 32)
                    if not start:
                        pe.wait_ge(hb_ready, n * ST + (i - 1))
                    for k in range(KT):
                        for w in range(2):
                            for wh, hh in ((0, 0), (0, 1), (1, 0)):
                                mm = pe.matmul(pG[x][w][:, :], wgu[:, i, k, w, wh, :],
                                               hT[u][:, :, k, hh, :], start=k == 0 and (wh, hh) == (0, 0),
                                               stop=k == KT - 1 and wh == 1)
                    mm.then_inc(gu_ps, 1)

                def down(n, i):
                    pe.wait_ge(s_low, n * ST + (i + 1))
                    if i == 0:
                        pe.wait_ge(y_read, n * SUB)
                    for t in range(SUB):
                        for sh, wh in ((0, 0), (0, 1), (1, 0)):
                            mm = pe.matmul(pY[t][:, :], sT[:, i, sh, t * P:(t + 1) * P], wdn[:, i, wh, :],
                                           start=i == 0 and (sh, wh) == (0, 0), stop=i == ST - 1 and sh == 1)
                    mm.then_inc(y_ps, 1)

                def tile(n, u, last, first=False):
                    for i in range(ST):
                        if i + 1 < ST:
                            gate_up(n, u, i + 1, first, first and i == 0)
                        elif not last:
                            gate_up(n + 1, 1 - u, 0)
                        down(n, i)

                gate_up(0, 0, 0, True, True)
                tile(0, 0, False, True)
                tile(1, 1, False)
                with pe.Fori(1, LATE // 2 - 1) as i:
                    tile(i * 2, 0, False)
                    tile(i * 2 + 1, 1, False)
                tile(LATE - 2, 0, False)
                tile(LATE - 1, 1, True)

            @block.scalar
            def _(act):
                def part(n, u, i):
                    x = (u * ST + i) % 2
                    act.wait_ge(gu_ps, n * ST + (i + 1))
                    act.activation(th[x][:, :], pG[x][0][:, :], ACT.Tanh, scale=0.5 / WS).then_inc(th_ready, 1)
                    act.wait_ge(hb_ready, n * ST + (i + 1))
                    act.activation(sT[:, i, 0, :], hb[x][:, :], ACT.Copy).then_inc(s_high, 1)

                with act.Fori(0, LATE // 2) as j:
                    for u in range(2):
                        for i in range(ST):
                            part(j * 2 + u, u, i)

            @block.vector
            def _(dve):
                def part(n, u, i):
                    x = (u * ST + i) % 2
                    at = n * ST + (i + 1)
                    dve.wait_ge(th_ready, at)
                    dve.scalar_tensor_tensor(gt[x][:, :], th[x][:, :], 1.0, pG[x][0][:, :], ALU.add, ALU.mult).then_inc(gt_ready, 1)
                    dve.wait_ge(gt_ready, at)
                    dve.scalar_tensor_tensor(hb[x][:, :], gt[x][:, :], 0.5 / (WS * WS), pG[x][1][:, :], ALU.mult, ALU.mult)\
                       .then_inc(hb_ready, 1)
                    dve.wait_ge(s_high, at)
                    dve.tensor_tensor(sT[:, i, 1, :], hb[x][:, :], sT[:, i, 0, :], ALU.subtract).then_inc(s_low, 1)

                def weigh(n, u, pair):
                    dve.wait_ge(stored[u], pair * 16)
                    dve.wait_ge(y_in, (n + 1) * (SUB * TOPK * 16))
                    for i in range(SUB):
                        at = n * SUB + i
                        dve.tensor_scalar(rt[u][:, i, :], yg[:, i, 0, :], ro.weights[:, 0, bass.ds(at + FIRST * SUB, 1)], None, ALU.mult)\
                           .then_inc(first_mix, 1)
                    for i in range(SUB):
                        at = n * SUB + i
                        if i == 0:
                            dve.wait_ge(first_mix, n * (2 * SUB) + SUB)
                        dve.scalar_tensor_tensor(rt[u][:, i, :], yg[:, i, 1, :], ro.weights[:, 1, bass.ds(at + FIRST * SUB, 1)], rt[u][:, i, :],
                                                 ALU.mult, ALU.add).then_inc(first_mix, 1)

                def add_shared(n, u):
                    b = (n + FIRST) // (S // TB)
                    dve.wait_ge(gb_in, B * 16)
                    dve.wait_ge(y_ps, (n + 1) * ST)
                    for i in range(SUB):
                        dve.scalar_tensor_tensor(sg[:, i, :], pY[i][:, :], ro.shared[:, bass.ds(n * SUB + (i + FIRST * SUB), 1)],
                                                 gb[:, bass.ds(b, 1), :].rearrange("p o d -> p (o d)"),
                                                 ALU.mult, ALU.mult).then_inc(y_read, 1)
                    dve.wait_ge(fin, (n + 1) * (2 * SUB))
                    for i in range(SUB):
                        dve.wait_ge(y_read, n * SUB + (i + 1))
                        dve.tensor_tensor(rt[u][:, i, :], rt[u][:, i, :], sg[:, i, :], ALU.add).then_inc(mixed, 1)

                def tile(n, u, pair, last):
                    for i in range(ST):
                        if i + 1 < ST:
                            part(n, u, i + 1)
                        elif not last:
                            part(n + 1, 1 - u, 0)
                        if i == MIX:
                            weigh(n, u, pair)
                    add_shared(n, u)

                part(0, 0, 0)
                with dve.Fori(0, LATE // 2 - 1) as j:
                    tile(j * 2, 0, j, False)
                    tile(j * 2 + 1, 1, j, False)
                tile(LATE - 2, 0, LATE // 2 - 1, False)
                tile(LATE - 1, 1, LATE // 2 - 1, True)


def adaln_block(nc, a, out):
    s = Scratch(nc)
    modulation_and_qkv(nc, a, s)
    with ExitStack() as ctx:
        ro = Routing(ctx, nc)
        with nc.sbuf_tensor("routed_w", [P, E, RWC], fp16) as rw:
            attention(nc, a, s, rw)
            project_and_route(nc, a, s, ro)
            choose_and_scatter(nc, s, ro)
            routed_experts(nc, s, ro, rw)
        shared_expert_and_sum(nc, a, s, ro, out)


_INS = ["L0_attn_x", "L0_attn_Wq", "L0_attn_Wk", "L0_attn_Wv", "L0_attn_Wo", "L0_ffn_router_w",
        "L0_ffn_w_gate", "L0_ffn_w_up", "L0_ffn_w_down", "L0_ffn_sw_gate", "L0_ffn_sw_up",
        "L0_ffn_sw_down", "L0_ffn_shared_gate_w", "L0_c", "L0_wmod"]


def kernel(**inputs):
    import numpy as np
    import concourse.bacc as bacc
    from concourse.bass_utils import run_bass_kernel_spmd

    nc = bacc.Bacc("TRN2", target_bir_lowering=False, num_devices=1)
    arrays, aps = {}, {}
    for name in _INS:
        arrays[name] = np.ascontiguousarray(inputs[name])
        aps[name] = nc.dram_tensor(name, arrays[name].shape, mybir.dt.from_np(arrays[name].dtype), kind="ExternalInput").ap()
    out = nc.dram_tensor("out", (B, S, D), fp32, kind="ExternalOutput").ap()
    adaln_block(nc, aps, out)
    r = run_bass_kernel_spmd(nc, [arrays], core_ids=[0])
    return r.results[0]["out"]
```
